# Optimizing a Trainium2 kernel written in Bass

```python
import numpy as np
import jax
import jax.numpy as jnp

def _softmax(x, axis=-1):
    return jax.nn.softmax(x, axis=axis)

def _gelu(x):
    return jax.nn.gelu(x, approximate=True)

def _silu(x):
    return jax.nn.silu(x)

def _sigmoid(x):
    return jax.nn.sigmoid(x)

def _layernorm(x, axis=-1, eps=1e-05):
    m = jnp.mean(x, axis=axis, keepdims=True)
    v = jnp.var(x, axis=axis, keepdims=True)
    return (x - m) / jnp.sqrt(v + eps)

def _scatter_add(tgt, idx, src, axis=0):
    return tgt.at[idx].add(src)

def _segment_sum(src, seg, n):
    return jax.ops.segment_sum(src, seg, n)
kernel_name = 'mk_audio_tower_d1_tok_audfeat1024_r4_6e97d2'

def setup_inputs(seed: int=0):
    np.random.seed(seed)
    _w = jnp.asarray

    def _rec_inputs():
        import jax
        import jax.numpy as jnp
        _rk = jax.random.key(seed)
        x = -0.000125008 + 0.999885 * jax.random.normal(jax.random.fold_in(_rk, 1), (64, 125, 256), jnp.float32)
        return x
    x = _rec_inputs()

    def _L0_tok_setup():
        import jax, jax.numpy as jnp
        import numpy as np
        D_MODEL = 256
        STRIDE = 2
        KERNEL = 2
        INIT_STD = 0.02
        EPS = 1e-05
        key = jax.random.key(seed)
        k1, k2 = jax.random.split(key)
        hidden_states = jax.random.normal(k1, (4, 2048, D_MODEL), dtype=jnp.float32)
        conv_w = INIT_STD * jax.random.normal(k2, (D_MODEL, D_MODEL, KERNEL), dtype=jnp.float32)
        conv_b = jnp.zeros((D_MODEL,), dtype=jnp.float32)
        ln_gamma = jnp.ones((D_MODEL,), dtype=jnp.float32)
        ln_beta = jnp.zeros((D_MODEL,), dtype=jnp.float32)
        return {'hidden_states': hidden_states, 'conv_w': conv_w, 'conv_b': conv_b, 'ln_gamma': ln_gamma, 'ln_beta': ln_beta}
    _L0_tok_all = _L0_tok_setup()
    _L0_tok_in = {k: v for k, v in _L0_tok_all.items() if k in ('conv_w', 'conv_b', 'ln_gamma', 'ln_beta')}
    del _L0_tok_all

    def _L0_attn_setup():
        import jax, jax.numpy as jnp
        import numpy as np
        B, S, IN_DIM, D_MODEL, NUM_HEADS = (4, 512, 256, 256, 16)
        HEAD_DIM = D_MODEL // NUM_HEADS
        CAUSAL = True
        NEG = -9000000000000000.0

        def _xavier(key, shape):
            fan_out, fan_in = shape
            limit = (6.0 / (fan_in + fan_out)) ** 0.5
            return jax.random.uniform(key, shape, jnp.float32, -limit, limit)
        key = jax.random.key(seed)
        ks = jax.random.split(key, 5)
        x = jax.random.normal(ks[0], (B, S, IN_DIM), jnp.float32)
        Wq = _xavier(ks[1], (D_MODEL, IN_DIM))
        Wk = _xavier(ks[2], (D_MODEL, IN_DIM))
        Wv = _xavier(ks[3], (D_MODEL, IN_DIM))
        Wo = _xavier(ks[4], (D_MODEL, D_MODEL))
        bq = jnp.zeros((D_MODEL,), jnp.float32)
        bk = jnp.zeros((D_MODEL,), jnp.float32)
        bv = jnp.zeros((D_MODEL,), jnp.float32)
        bo = jnp.zeros((D_MODEL,), jnp.float32)
        return {'x': x, 'Wq': Wq, 'bq': bq, 'Wk': Wk, 'bk': bk, 'Wv': Wv, 'bv': bv, 'Wo': Wo, 'bo': bo}
    _L0_attn_all = _L0_attn_setup()
    _L0_attn_in = {k: v for k, v in _L0_attn_all.items() if k in ('Wq', 'bq', 'Wk', 'bk', 'Wv', 'bv', 'Wo', 'bo')}
    del _L0_attn_all

    def _L0_ffn_setup():
        import jax, jax.numpy as jnp
        import numpy as np
        D = 256
        H = 16
        FF = 1024
        E = 8
        K = 2
        EH = 256
        B, S = (2, 512)
        EPS = 1e-05

        def rmsnorm(x, w):
            v = jnp.mean(jnp.square(x), axis=-1, keepdims=True)
            return x * jax.lax.rsqrt(v + EPS) * w

        def _dense_path(x, wq, wk, wv, wo, w1, w2, w3, attn_norm_w, ff_norm_w):
            b, s, d = x.shape
            hd = d // H
            q = (x @ wq).reshape(b, s, H, hd)
            k = (x @ wk).reshape(b, s, H, hd)
            v = (x @ wv).reshape(b, s, H, hd)
            scores = jnp.einsum('bqhd,bkhd->bhqk', q, k) / np.sqrt(hd).astype(np.float32)
            causal = jnp.tril(jnp.ones((s, s), bool))
            scores = jnp.where(causal, scores, jnp.finfo(scores.dtype).min)
            attn = jax.nn.softmax(scores, axis=-1)
            o = jnp.einsum('bhqk,bkhd->bqhd', attn, v).reshape(b, s, d)
            h = x + rmsnorm(o @ wo, attn_norm_w)
            ffn = jax.nn.silu(h @ w1) * (h @ w3) @ w2
            return h + rmsnorm(ffn, ff_norm_w)

        def _sparse_path(x, router_w, ew1, ew2, ew3, moe_norm_w):
            b, s, d = x.shape
            xt = x.reshape(-1, d)
            probs = jax.nn.softmax(xt @ router_w, axis=-1)
            topw, topi = jax.lax.top_k(probs, K)
            g = jax.nn.silu(jnp.einsum('td,edh->eth', xt, ew1)) * jnp.einsum('td,edh->eth', xt, ew3)
            eo = jnp.einsum('eth,ehd->ted', g, ew2)
            sel = jnp.take_along_axis(eo, topi[:, :, None], axis=1)
            moe_out = jnp.sum(topw[:, :, None] * sel, axis=1).reshape(b, s, d)
            return rmsnorm(moe_out, moe_norm_w)
        key = jax.random.key(seed)
        ks = jax.random.split(key, 16)
        s = 0.02
        return {'x': jax.random.normal(ks[0], (B, S, D), jnp.float32), 'wq': jax.random.normal(ks[1], (D, D), jnp.float32) * s, 'wk': jax.random.normal(ks[2], (D, D), jnp.float32) * s, 'wv': jax.random.normal(ks[3], (D, D), jnp.float32) * s, 'wo': jax.random.normal(ks[4], (D, D), jnp.float32) * s, 'w1': jax.random.normal(ks[5], (D, FF), jnp.float32) * s, 'w2': jax.random.normal(ks[6], (FF, D), jnp.float32) * s, 'w3': jax.random.normal(ks[7], (D, FF), jnp.float32) * s, 'attn_norm_w': jnp.ones((D,), jnp.float32), 'ff_norm_w': jnp.ones((D,), jnp.float32), 'moe_norm_w': jnp.ones((D,), jnp.float32), 'router_w': jax.random.normal(ks[8], (D, E), jnp.float32) * s, 'ew1': jax.random.normal(ks[9], (E, D, EH), jnp.float32) * s, 'ew2': jax.random.normal(ks[10], (E, EH, D), jnp.float32) * s, 'ew3': jax.random.normal(ks[11], (E, D, EH), jnp.float32) * s}
    _L0_ffn_all = _L0_ffn_setup()
    _L0_ffn_in = {k: v for k, v in _L0_ffn_all.items() if k in ('wq', 'wk', 'wv', 'wo', 'w1', 'w2', 'w3', 'attn_norm_w', 'ff_norm_w', 'moe_norm_w', 'router_w', 'ew1', 'ew2', 'ew3')}
    del _L0_ffn_all
    return {'x': x, 'L0_tok_conv_w': _L0_tok_in['conv_w'], 'L0_tok_conv_b': _L0_tok_in['conv_b'], 'L0_tok_ln_gamma': _L0_tok_in['ln_gamma'], 'L0_tok_ln_beta': _L0_tok_in['ln_beta'], 'L0_attn_Wq': _L0_attn_in['Wq'], 'L0_attn_bq': _L0_attn_in['bq'], 'L0_attn_Wk': _L0_attn_in['Wk'], 'L0_attn_bk': _L0_attn_in['bk'], 'L0_attn_Wv': _L0_attn_in['Wv'], 'L0_attn_bv': _L0_attn_in['bv'], 'L0_attn_Wo': _L0_attn_in['Wo'], 'L0_attn_bo': _L0_attn_in['bo'], 'L0_ffn_wq': _L0_ffn_in['wq'], 'L0_ffn_wk': _L0_ffn_in['wk'], 'L0_ffn_wv': _L0_ffn_in['wv'], 'L0_ffn_wo': _L0_ffn_in['wo'], 'L0_ffn_w1': _L0_ffn_in['w1'], 'L0_ffn_w2': _L0_ffn_in['w2'], 'L0_ffn_w3': _L0_ffn_in['w3'], 'L0_ffn_attn_norm_w': _L0_ffn_in['attn_norm_w'], 'L0_ffn_ff_norm_w': _L0_ffn_in['ff_norm_w'], 'L0_ffn_moe_norm_w': _L0_ffn_in['moe_norm_w'], 'L0_ffn_router_w': _L0_ffn_in['router_w'], 'L0_ffn_ew1': _L0_ffn_in['ew1'], 'L0_ffn_ew2': _L0_ffn_in['ew2'], 'L0_ffn_ew3': _L0_ffn_in['ew3']}

def reference(x, L0_tok_conv_w, L0_tok_conv_b, L0_tok_ln_gamma, L0_tok_ln_beta, L0_attn_Wq, L0_attn_bq, L0_attn_Wk, L0_attn_bk, L0_attn_Wv, L0_attn_bv, L0_attn_Wo, L0_attn_bo, L0_ffn_wq, L0_ffn_wk, L0_ffn_wv, L0_ffn_wo, L0_ffn_w1, L0_ffn_w2, L0_ffn_w3, L0_ffn_attn_norm_w, L0_ffn_ff_norm_w, L0_ffn_moe_norm_w, L0_ffn_router_w, L0_ffn_ew1, L0_ffn_ew2, L0_ffn_ew3):
    import jax
    import jax.numpy as jnp

    def _L0_tok_ref(hidden_states, conv_w, conv_b, ln_gamma, ln_beta):
        import jax, jax.numpy as jnp
        import numpy as np
        D_MODEL = 256
        STRIDE = 2
        KERNEL = 2
        INIT_STD = 0.02
        EPS = 1e-05
        B, L, D = hidden_states.shape
        pad_len = -L % STRIDE
        if pad_len:
            hidden_states = jnp.pad(hidden_states, ((0, 0), (0, pad_len), (0, 0)))
            L = L + pad_len
        xb = hidden_states.reshape(B, L // STRIDE, STRIDE, D)
        x = jnp.einsum('btki,oik->bto', xb, conv_w) + conv_b
        x = x + xb.mean(axis=2)
        mu = x.mean(axis=-1, keepdims=True)
        var = jnp.mean(jnp.square(x - mu), axis=-1, keepdims=True)
        x = (x - mu) * jax.lax.rsqrt(var + EPS) * ln_gamma + ln_beta
        return x

    def _L0_attn_ref(x, Wq, bq, Wk, bk, Wv, bv, Wo, bo):
        import jax, jax.numpy as jnp
        import numpy as np
        B, S, IN_DIM, D_MODEL, NUM_HEADS = (4, 512, 256, 256, 16)
        HEAD_DIM = D_MODEL // NUM_HEADS
        CAUSAL = True
        NEG = -9000000000000000.0

        def _xavier(key, shape):
            fan_out, fan_in = shape
            limit = (6.0 / (fan_in + fan_out)) ** 0.5
            return jax.random.uniform(key, shape, jnp.float32, -limit, limit)
        batch, seq, _ = x.shape
        q = x @ Wq.T + bq
        k = x @ Wk.T + bk
        v = x @ Wv.T + bv

        def split(t):
            return t.reshape(batch, seq, NUM_HEADS, HEAD_DIM).transpose(0, 2, 1, 3)
        q, k, v = (split(q), split(k), split(v))
        scores = jnp.einsum('bhqd,bhkd->bhqk', q, k) / jnp.sqrt(jnp.float32(HEAD_DIM))
        if CAUSAL:
            mask = jnp.tril(jnp.ones((seq, seq), bool))
            scores = jnp.where(mask, scores, jnp.float32(NEG))
        attn = jax.nn.softmax(scores, axis=-1)
        out = jnp.einsum('bhqk,bhkd->bhqd', attn, v)
        out = out.transpose(0, 2, 1, 3).reshape(batch, seq, D_MODEL)
        return out @ Wo.T + bo

    def _L0_ffn_ref(x, wq, wk, wv, wo, w1, w2, w3, attn_norm_w, ff_norm_w, moe_norm_w, router_w, ew1, ew2, ew3):
        import jax, jax.numpy as jnp
        import numpy as np
        D = 256
        H = 16
        FF = 1024
        E = 8
        K = 2
        EH = 256
        B, S = (2, 512)
        EPS = 1e-05

        def rmsnorm(x, w):
            v = jnp.mean(jnp.square(x), axis=-1, keepdims=True)
            return x * jax.lax.rsqrt(v + EPS) * w

        def _dense_path(x, wq, wk, wv, wo, w1, w2, w3, attn_norm_w, ff_norm_w):
            b, s, d = x.shape
            hd = d // H
            q = (x @ wq).reshape(b, s, H, hd)
            k = (x @ wk).reshape(b, s, H, hd)
            v = (x @ wv).reshape(b, s, H, hd)
            scores = jnp.einsum('bqhd,bkhd->bhqk', q, k) / np.sqrt(hd).astype(np.float32)
            causal = jnp.tril(jnp.ones((s, s), bool))
            scores = jnp.where(causal, scores, jnp.finfo(scores.dtype).min)
            attn = jax.nn.softmax(scores, axis=-1)
            o = jnp.einsum('bhqk,bkhd->bqhd', attn, v).reshape(b, s, d)
            h = x + rmsnorm(o @ wo, attn_norm_w)
            ffn = jax.nn.silu(h @ w1) * (h @ w3) @ w2
            return h + rmsnorm(ffn, ff_norm_w)

        def _sparse_path(x, router_w, ew1, ew2, ew3, moe_norm_w):
            b, s, d = x.shape
            xt = x.reshape(-1, d)
            probs = jax.nn.softmax(xt @ router_w, axis=-1)
            topw, topi = jax.lax.top_k(probs, K)
            g = jax.nn.silu(jnp.einsum('td,edh->eth', xt, ew1)) * jnp.einsum('td,edh->eth', xt, ew3)
            eo = jnp.einsum('eth,ehd->ted', g, ew2)
            sel = jnp.take_along_axis(eo, topi[:, :, None], axis=1)
            moe_out = jnp.sum(topw[:, :, None] * sel, axis=1).reshape(b, s, d)
            return rmsnorm(moe_out, moe_norm_w)
        dense_out = _dense_path(x, wq, wk, wv, wo, w1, w2, w3, attn_norm_w, ff_norm_w)
        sparse_out = _sparse_path(x, router_w, ew1, ew2, ew3, moe_norm_w)
        return dense_out + sparse_out
    h = _L0_tok_ref(x, L0_tok_conv_w, L0_tok_conv_b, L0_tok_ln_gamma, L0_tok_ln_beta)
    h = h + _L0_attn_ref(_layernorm(h, axis=-1), L0_attn_Wq, L0_attn_bq, L0_attn_Wk, L0_attn_bk, L0_attn_Wv, L0_attn_bv, L0_attn_Wo, L0_attn_bo)
    h = h + _L0_ffn_ref(_layernorm(h, axis=-1), L0_ffn_wq, L0_ffn_wk, L0_ffn_wv, L0_ffn_wo, L0_ffn_w1, L0_ffn_w2, L0_ffn_w3, L0_ffn_attn_norm_w, L0_ffn_ff_norm_w, L0_ffn_moe_norm_w, L0_ffn_router_w, L0_ffn_ew1, L0_ffn_ew2, L0_ffn_ew3)
    return h

_drawn_inputs = setup_inputs


def setup_inputs(seed=0):
    import zlib

    import numpy as np

    out = dict(_drawn_inputs(seed))
    spreads = {'L0_tok_conv_b': (0.0, 0.1),
     'L0_tok_ln_gamma': (1.0, 0.2),
     'L0_tok_ln_beta': (0.0, 0.1),
     'L0_attn_bq': (0.0, 0.1),
     'L0_attn_bk': (0.0, 0.1),
     'L0_attn_bv': (0.0, 0.1),
     'L0_attn_bo': (0.0, 0.1),
     'L0_ffn_attn_norm_w': (1.0, 0.2),
     'L0_ffn_ff_norm_w': (1.0, 0.2),
     'L0_ffn_moe_norm_w': (1.0, 0.2)}
    factors = {}
    for name, (base, spread) in spreads.items():
        noise = np.random.default_rng([zlib.crc32(name.encode()), seed]).standard_normal(out[name].shape)
        drawn = base * np.exp(spread * noise) if base else spread * noise
        out[name] = jnp.asarray(drawn.astype(out[name].dtype))
    for name, factor in factors.items():
        out[name] = (out[name] * factor).astype(out[name].dtype)
    return out
```

```python
from contextlib import ExitStack

import concourse.bass as bass
from concourse import mybir

F32 = mybir.dt.float32
ACT = mybir.ActivationFunctionType
ALU = mybir.AluOpType
AX = mybir.AxisListType.X

P = 128
B, L, D = 64, 125, 256
TOK = (L + 1) // 2
SLOT = 64
T = 4
G = B // (2 * T)
C = D // P
GT = T * P
H, HD = 16, 16
VW = HD + 1
FF, E = 1024, 8
UE = E * 2
UD = FF // P
U = UE + UD
XC = 2 * D // P
EPS = 1e-5
NEG = -1e30
QSCALE = HD ** -0.5

ATT, DENSE, MOE = range(3)
DOWNS = E + UD
PRIME = 1
LINKS = 61

CONV_B, GAMMA, BETA, BV, BO, W_ATT, W_FF, W_MOE = range(8)
BQ, BK, MEVEN, MODD = 0, 2, 4, 5


def program(nc, x, rows, cols, ident_in, mask_in, lower_in, conv_w, attn_w, w1_in, w3_in, w2_in, router_in,
            ew1_in, ew3_in, ew2_in, out):
    ctx = ExitStack()
    with ctx:
        def sb(name, shape):
            return ctx.enter_context(nc.sbuf_tensor(name, shape, F32))

        def sem(name):
            return ctx.enter_context(nc.semaphore(name))

        convw = sb("convw", [P, XC, D])
        attnw = sb("attnw", [P, 8, C, D])
        w1 = sb("w1", [P, C, FF])
        w3 = sb("w3", [P, C, FF])
        w2 = sb("w2", [P, UD, D])
        ew1 = sb("ew1", [P, E, C, D])
        ew3 = sb("ew3", [P, E, C, D])
        ew2 = sb("ew2", [P, E, C, D])
        router = sb("router", [P, C, E])
        rowv = sb("rowv", [P, 8, D])
        colv = sb("colv", [P, 6])
        bqs = sb("bqs", [P, C])
        ident = sb("ident", [P, P])
        mask = sb("mask", [P, SLOT])
        lower = sb("lower", [P, E * E])
        x_in = sb("x_in", [P, T, 2 * D])
        xT = sb("xT", [P, XC, GT])
        h = sb("h", [P, T, D])
        n = sb("n", [P, T, D])
        hd = sb("hd", [P, T, D])
        nT = sb("nT", [P, C, GT])
        hdT = xT[:, 0:C, :]
        qT = sb("qT", [P, C, GT])
        kT = sb("kT", [P, C, 2, GT])
        v = sb("v", [P, T, H, VW])
        scores = sb("scores", [P, 2, H, SLOT])
        probs = sb("probs", [P, 2, H, 2 * SLOT])
        pT = sb("pT", [P, 2, T * P])
        o = sb("o", [P, T, D])
        oT = sb("oT", [P, C, GT])
        gate = sb("gate", [P, 2, GT])
        up = sb("up", [P, 2, GT])
        hidT = scores[:, :, :, :].rearrange("p a h k -> p (a h k)").rearrange("p (u r) -> p u r", u=4)
        moe = sb("moe", [P, T, D])
        y = sb("y", [P, T, D])

        def squares(j):
            return xT[:, C + j // 2, D * (j % 2):D * (j % 2) + D]

        bst = sb("bst", [P, T, 6])
        mv = sb("mv", [P, T, 2])
        vare = sb("vare", [P, T])
        rstd = sb("rstd", [P, T])
        fence = sb("fence", [P, 1])
        nhalf = sb("nhalf", [P, T])
        epsv = sb("epsv", [P, T])
        ss = sb("ss", [P, 3, T])
        msq = sb("msq", [P, 3, T])
        rms = sb("rms", [P, 3, T])
        mx = sb("mx", [P, H])
        rinv = sb("rinv", [P, H])
        lg = sb("lg", [P, T, E])
        pr = sb("pr", [P, T, E])
        rs = sb("rs", [P, T])
        gt = sb("gt", [P, T * E, E])
        eq = sb("eq", [P, T * E, E])
        rank = sb("rank", [P, T, E])
        cw = sb("cw", [P, T, E])

        ps = ctx.enter_context(nc.psum_tensor("ps", [P, 8, 512], F32))

        s_w = [sem(f"s_w{i}") for i in range(4)]
        s_x = sem("s_x")
        s_setup = sem("s_setup")
        s_pad = sem("s_pad")
        s_const = sem("s_const")
        s_fold = sem("s_fold")
        s_xt_ps = sem("s_xt_ps")
        s_xt_a = sem("s_xt_a")
        s_xt_v = sem("s_xt_v")
        s_conv = sem("s_conv")
        s_order = sem("s_order")
        s_var = sem("s_var")
        s_vare = sem("s_vare")
        s_rstd = sem("s_rstd")
        s_hn = sem("s_hn")
        s_n = sem("s_n")
        s_hbo = sem("s_hbo")
        s_nT_ps = sem("s_nT_ps")
        s_nT_a = sem("s_nT_a")
        s_nT_v = sem("s_nT_v")
        s_qk_ps = sem("s_qk_ps")
        s_q = sem("s_q")
        s_k = sem("s_k")
        s_v_ps = sem("s_v_ps")
        s_v0 = sem("s_v0")
        s_v1 = sem("s_v1")
        s_s_ps = sem("s_s_ps")
        s_s_read = sem("s_s_read")
        s_s_sub = sem("s_s_sub")
        s_p = sem("s_p")
        s_pT_ps = sem("s_pT_ps")
        s_pT_a = sem("s_pT_a")
        s_pT_v = sem("s_pT_v")
        s_pv = sem("s_pv")
        s_o = sem("s_o")
        s_oT_ps = sem("s_oT_ps")
        s_oT_a = sem("s_oT_a")
        s_oT_v = sem("s_oT_v")
        s_wo = sem("s_wo")
        s_h2 = sem("s_h2")
        s_ss = sem("s_ss")
        s_msq = sem("s_msq")
        s_rms = sem("s_rms")
        s_hd = sem("s_hd")
        s_lg_ps = sem("s_lg_ps")
        s_lgs = sem("s_lgs")
        s_lge = sem("s_lge")
        s_hdT_ps = sem("s_hdT_ps")
        s_hdT_a = sem("s_hdT_a")
        s_hdT_v = sem("s_hdT_v")
        s_up_ps = sem("s_up_ps")
        s_gate = sem("s_gate")
        s_hid = sem("s_hid")
        s_down = sem("s_down")
        s_moe = sem("s_moe")
        s_fd = sem("s_fd")
        s_y = sem("s_y")
        s_out = sem("s_out")

        block = ctx.enter_context(nc.Block())

        def head(r, c, e):
            return 8 * c + 2 * r + e

        @block.sync
        def _(sp):
            def load_x(g):
                for s in range(2):
                    src = x[g, :, s]
                    sp.dma_start(x_in[SLOT * s:SLOT * s + TOK - 1, :, :],
                                 src[:, 0:L - 1, :].rearrange("j (t k) i -> t j (k i)", k=2)).then_inc(s_x, 16)
                    sp.dma_start(x_in[SLOT * s + TOK - 1:SLOT * s + TOK, :, 0:D],
                                 src[:, L - 1:L, :].rearrange("j t i -> t j i")).then_inc(s_x, 16)

            def store_y(g):
                for s in range(2):
                    sp.dma_start(out[g, :, s].rearrange("j t i -> t j i"),
                                 y[SLOT * s:SLOT * s + TOK, :, :]).then_inc(s_out, 16)

            sp.dma_start(ident[:], ident_in).then_inc(s_w[0], 16)
            sp.dma_start(mask[:], mask_in).then_inc(s_w[0], 16)
            sp.dma_start(lower[:], lower_in).then_inc(s_w[0], 16)
            sp.dma_start(colv[:], cols).then_inc(s_w[0], 16)
            sp.dma_start(rowv[:], rows).then_inc(s_w[0], 16)
            sp.wait_ge(s_pad, 2)
            load_x(0)
            sp.dma_start(convw[:], conv_w).then_inc(s_w[1], 16)
            sp.dma_start(attnw[:], attn_w).then_inc(s_w[1], 16)
            sp.dma_start(router[:], router_in).then_inc(s_w[2], 16)
            sp.dma_start(ew1[:], ew1_in).then_inc(s_w[2], 16)
            sp.dma_start(ew3[:], ew3_in).then_inc(s_w[2], 16)
            sp.dma_start(ew2[:], ew2_in).then_inc(s_w[2], 16)
            sp.dma_start(w1[:], w1_in).then_inc(s_w[3], 16)
            sp.dma_start(w3[:], w3_in).then_inc(s_w[3], 16)
            sp.dma_start(w2[:], w2_in).then_inc(s_w[3], 16)
            sp.sem_inc(s_out, PRIME)
            with sp.Fori(0, G - 1) as g:
                sp.wait_ge(s_xt_ps, g * XC + XC)
                load_x(g + 1)
                sp.wait_ge(s_y, g + 1)
                store_y(g)
            sp.wait_ge(s_y, G)
            store_y(G - 1)
            sp.wait_ge(s_out, PRIME + G * 32)

        @block.gpsimd
        def _(pool):
            pool.memset(x_in[:, 0:2, :], 0.0).then_inc(s_pad, 1)
            pool.memset(x_in[:, 2:4, :], 0.0).then_inc(s_pad, 1)
            pool.memset(nhalf[:], -0.5).then_inc(s_const, 1)
            pool.memset(epsv[:], EPS).then_inc(s_const, 1)
            pool.wait_ge(s_const, 2)
            pool.wait_ge(s_w[0], 80)
            with pool.Fori(0, G) as g:
                def power(k):
                    pool.wait_ge(s_var, g * 3 + k + 1)
                    pool.tensor_tensor(vare[:], mv[:, :, 1], epsv[:], ALU.add).then_inc(s_vare, 1)
                    pool.wait_ge(s_vare, g * 3 + k + 1)
                    pool.tensor_tensor(rstd[:], vare[:], nhalf[:], ALU.pow).then_inc(s_rstd, 1)

                def rms_power(k, at):
                    pool.wait_ge(s_ss, PRIME + g * (3 * T) + T * (k + 1))
                    pool.tensor_tensor(msq[:, at, :], ss[:, at, :], epsv[:], ALU.add).then_inc(s_msq, 1)
                    pool.wait_ge(s_msq, g * 3 + k + 1)
                    pool.tensor_tensor(rms[:, at, :], msq[:, at, :], nhalf[:], ALU.pow).then_inc(s_rms, 1)

                power(0)
                power(1)
                pool.wait_ge(s_n, g * (2 * T) + T)
                pool.tensor_tensor(h[:], h[:], rowv[:, BO:BO + 1, :].broadcast_to([P, T, D]), ALU.add).then_inc(s_hbo, 1)
                power(2)
                rms_power(0, ATT)
                rms_power(1, MOE)
                rms_power(2, DENSE)

        @block.scalar
        def _(act):
            act.wait_ge(s_w[0], 80)
            act.wait_ge(s_setup, 4)
            act.sem_inc(s_ss, PRIME)
            with act.Fori(0, G) as g:
                act.wait_ge(s_ss, PRIME + g * (3 * T))
                for c in range(0, XC, 2):
                    act.wait_ge(s_xt_ps, g * XC + c + 1)
                    act.activation(xT[:, c, :], ps[:, c, :], ACT.Copy).then_inc(s_xt_a, 1)
                for a in range(2):
                    act.wait_ge(s_nT_ps, g * 4 + 2 * a + 1)
                    act.activation(nT[:, 0, :], ps[:, 0, :], ACT.Copy).then_inc(s_nT_a, 1)
                    for c in range(C):
                        act.wait_ge(s_qk_ps, g * 8 + 4 * a + c + 1)
                        bias = bqs[:, c:c + 1] if a == 0 else 0.0
                        act.activation(qT[:, c, :], ps[:, 2 + c, :], ACT.Identity, bias=bias, scale=QSCALE).then_inc(s_q, 1)
                    if a == 1:
                        for j in range(T):
                            act.wait_ge(s_v_ps, g * 8 + 4 * a + j + 1)
                            act.activation(v[:, j, :, 0:HD], ps[:, (6 + j) % 8, 0:D].rearrange("p (h d) -> p h d", d=HD),
                                           ACT.Copy).then_inc(s_v1, 1)

                    def exps(j):
                        k = 4 * a + j
                        act.wait_ge(s_s_sub, g * 8 + k + 1)
                        if k >= 2:
                            act.wait_ge(s_pT_ps, g * 32 + 4 * (k - 1))
                        for s in range(2):
                            rows = slice(SLOT * s, SLOT * s + SLOT)
                            act.activation(probs[rows, j % 2, :, SLOT * s:SLOT * s + SLOT], scores[rows, j % 2, :, :],
                                           ACT.Exp).then_inc(s_p, 1)

                    def evac(j):
                        for q in range(4):
                            k = 4 * (4 * a + j) + q
                            act.wait_ge(s_pT_ps, g * 32 + k + 1)
                            if k >= 2:
                                act.wait_ge(s_pv, g * 32 + k - 1)
                            act.activation(pT[:, q % 2, :], ps[:, 4 + q % 2, :], ACT.Copy).then_inc(s_pT_a, 1)

                    exps(0)
                    for j in range(T):
                        if j + 1 < T:
                            exps(j + 1)
                        if a == 1 and j == 1:
                            act.wait_ge(s_lgs, g + 1)
                            act.activation(lg[:], lg[:], ACT.Exp).then_inc(s_lge, 1)
                        evac(j)
                    act.wait_ge(s_oT_ps, g * 4 + 2 * a + 1)
                    act.activation(oT[:, 0, :], ps[:, 0, :], ACT.Copy).then_inc(s_oT_a, 1)
                for j in range(T):
                    act.wait_ge(s_wo, g * 8 + T + j + 1)
                    act.activation(squares(j), ps[:, 4 + j, 0:D], ACT.Square, scale=D ** -0.5, accum_out=ss[:, ATT, j:j + 1]).then_inc(s_ss, 1)

                def gates(i):
                    act.wait_ge(s_up_ps, g * U + i + 1)
                    if i >= 2:
                        act.wait_ge(s_hid, PRIME + g * U + i - 1)
                    act.activation(gate[:, i % 2, :], ps[:, 2 * (i % 2), :], ACT.Tanh, scale=0.5).then_inc(s_gate, 1)

                for i in range(U):
                    if i == UE:
                        act.wait_ge(s_hdT_ps, g * 2 + 1)
                        act.activation(hdT[:, 0, :], ps[:, 0, :], ACT.Copy).then_inc(s_hdT_a, 1)
                    gates(i)
                    if i == UE + 1:
                        act.wait_ge(s_moe, g * E + E)
                        for j in range(T):
                            act.activation(o[:, j, :], moe[:, j, :], ACT.Square, scale=D ** -0.5, accum_out=ss[:, MOE, j:j + 1]).then_inc(s_ss, 1)
                act.wait_ge(s_down, PRIME + g * DOWNS + DOWNS)
                for j in range(T):
                    act.activation(squares(j), ps[:, 4 + j, 0:D], ACT.Square, scale=D ** -0.5, accum_out=ss[:, DENSE, j:j + 1]).then_inc(s_ss, 1)

        @block.tensor
        def _(pe):
            pe.wait_ge(s_w[0], 80)
            pe.wait_ge(s_setup, 4)
            pe.wait_ge(s_fold, 1)
            pe.wait_ge(s_w[1], 32)
            pe.wait_ge(s_w[2], 64)
            pe.wait_ge(s_w[3], 48)

            def project(dst, left, right, rows, chunks):
                for c in range(chunks):
                    mm = pe.matmul(dst, left(c), right(c), start=(c == 0), stop=(c == chunks - 1))
                return mm

            pe.sem_inc(s_down, PRIME)
            with pe.Fori(0, G) as g:
                pe.wait_ge(s_x, g * 64 + 64)
                pe.wait_ge(s_hid, PRIME + g * U)
                for c in range(XC):
                    for j in range(T):
                        mm = pe.transpose(ps[:, c, P * j:P * j + P], x_in[:, j, P * c:P * c + P], ident[:])
                    mm.then_inc(s_xt_ps, 1)
                pe.wait_ge(s_xt_a, g * 2 + 2)
                pe.wait_ge(s_xt_v, g * 2 + 2)
                pe.wait_ge(s_fd, PRIME + g * T)
                for j in range(T):
                    project(ps[:, 4 + j, 0:D], lambda c: xT[:, c, P * j:P * j + P], lambda c: convw[:, c, :], P, XC)\
                        .then_inc(s_conv, 1)

                def turn(src, bank, done):
                    for c in range(C):
                        for j in range(T):
                            mm = pe.transpose(ps[:, bank + c, P * j:P * j + P], src[:, j, P * c:P * c + P], ident[:])
                        mm.then_inc(done, 1)

                for a in range(2):
                    wq, wk, wv, wo = (attnw[:, 4 * a + i, :, :] for i in range(4))
                    pe.wait_ge(s_n, g * (2 * T) + T * (a + 1))
                    turn(n, 0, s_nT_ps)
                    pe.wait_ge(s_nT_a, g * 2 + a + 1)
                    pe.wait_ge(s_nT_v, g * 2 + a + 1)
                    for w, bank in ((wq, 2), (wk, 4)):
                        for c in range(C):
                            project(ps[:, bank + c, :], lambda k: w[:, k, P * c:P * c + P], lambda k: nT[:, k, :], P, C)\
                                .then_inc(s_qk_ps, 1)
                    for j in range(T):
                        project(ps[:, (6 + j) % 8, 0:D], lambda k: nT[:, k, P * j:P * j + P], lambda k: wv[:, k, :], P, C)\
                            .then_inc(s_v_ps, 1)

                    def score(j):
                        k = 4 * a + j
                        if j == 0:
                            pe.wait_ge(s_q, g * 4 + 2 * a + 2)
                            pe.wait_ge(s_k, g * 4 + 2 * a + 2)
                            pe.wait_ge(s_v1 if a else s_v0, g * 4 + 4)
                        else:
                            pe.wait_ge(s_s_read, g * 8 + k)
                        for r in range(4):
                            rows = slice(32 * r, 32 * r + 32)
                            for c in range(C):
                                for s in range(2):
                                    at = P * j + SLOT * s
                                    dst = ps[SLOT * s:SLOT * s + SLOT, r, 2 * SLOT * c:2 * SLOT * (c + 1)]
                                    mm = pe.matmul(dst.rearrange("p (e k) -> p e k", e=2), qT[rows, c, at:at + SLOT],
                                                   kT[rows, c, :, at:at + SLOT], start=True, stop=True)
                        mm.then_inc(s_s_ps, 1)

                    def weigh(j):
                        k = 4 * a + j
                        pe.wait_ge(s_p, g * 16 + 2 * k + 2)
                        for q in range(4):
                            if 4 * k + q >= 2:
                                pe.wait_ge(s_pT_a, g * 32 + 4 * k + q - 1)
                            for i in range(4):
                                mm = pe.transpose(ps[:, 4 + q % 2, P * i:P * i + P], probs[:, j % 2, 4 * q + i, :], ident[:])
                            mm.then_inc(s_pT_ps, 1)
                            if q >= 1:
                                values(j, q - 1)
                        values(j, 3)

                    def values(j, q):
                        k = 4 * a + j
                        pe.wait_ge(s_pT_a, g * 32 + 4 * k + q + 1)
                        if q == 0 and j >= 1:
                            pe.wait_ge(s_o, g * 8 + k)
                        for i in range(4):
                            at = head(q, i // 2, i % 2)
                            mm = pe.matmul(ps[:, 6, VW * at:VW * at + VW], pT[:, q % 2, P * i:P * i + P], v[:, j, at, :],
                                           start=True, stop=True)
                        mm.then_inc(s_pv, 1)

                    score(0)
                    if a == 1:
                        for j in range(T):
                            mm = project(ps[:, 7, E * j:E * j + E], lambda k: nT[:, k, P * j:P * j + P],
                                         lambda k: router[:, k, :], P, C)
                        mm.then_inc(s_lg_ps, 1)
                    for j in range(T):
                        if j + 1 < T:
                            score(j + 1)
                        weigh(j)
                    pe.wait_ge(s_o, g * 8 + 4 * a + 4)
                    turn(o, 0, s_oT_ps)
                    pe.wait_ge(s_oT_a, g * 2 + a + 1)
                    pe.wait_ge(s_oT_v, g * 2 + a + 1)
                    if a == 1:
                        pe.wait_ge(s_lgs, g + 1)
                    for j in range(T):
                        project(ps[:, 4 + j, 0:D], lambda k: oT[:, k, P * j:P * j + P], lambda k: wo[:, k, :], P, C)\
                            .then_inc(s_wo, 1)

                def ups(i):
                    if i >= 2:
                        pe.wait_ge(s_hid, PRIME + g * U + i - 1)
                    for which, bank in ((0, 0), (1, 1)):
                        if i < UE:
                            w = (ew1, ew3)[which][:, i // 2, :, P * (i % 2):P * (i % 2) + P]
                            src = nT
                        else:
                            w = (w1, w3)[which][:, :, P * (i - UE):P * (i - UE) + P]
                            src = hdT
                        mm = project(ps[:, 2 * (i % 2) + bank, :], lambda k: w[:, k, :], lambda k: src[:, k, :], P, C)
                    mm.then_inc(s_up_ps, 1)

                def down_expert(e):
                    pe.wait_ge(s_hid, PRIME + g * U + 2 * e + 2)
                    if e == 0:
                        pe.wait_ge(s_hd, g + 1)
                    if e >= 2:
                        pe.wait_ge(s_moe, g * E + e - 1)
                    for j in range(T):
                        mm = project(ps[:, 4 + 2 * (e % 2) + j // 2, D * (j % 2):D * (j % 2) + D],
                                     lambda k: hidT[:, (2 * e + k) % 4, P * j:P * j + P], lambda k: ew2[:, e, k, :], P, C)
                    mm.then_inc(s_down, 1)

                def down_dense(d):
                    pe.wait_ge(s_hid, PRIME + g * U + UE + d + 1)
                    if d == 0:
                        pe.wait_ge(s_moe, g * E + E)
                    for j in range(T):
                        mm = pe.matmul(ps[:, 4 + j, 0:D], hidT[:, d % 4, P * j:P * j + P], w2[:, d, :],
                                       start=(d == 0), stop=(d == UD - 1))
                    mm.then_inc(s_down, 1)

                ups(0)
                for e in range(E):
                    ups(2 * e + 1)
                    if e < E - 1:
                        ups(2 * e + 2)
                        down_expert(e)
                pe.wait_ge(s_hid, PRIME + g * U + UE - 1)
                turn(hd, 0, s_hdT_ps)
                down_expert(E - 1)
                pe.wait_ge(s_hdT_a, g + 1)
                pe.wait_ge(s_hdT_v, g + 1)
                ups(UE)
                for d in range(UD):
                    if d + 1 < UD:
                        ups(UE + d + 1)
                    down_dense(d)

        @block.vector
        def _(dve):
            order = [0]
            base = 3

            dve.memset(probs[:, 0, :, :], 0.0).then_inc(s_setup, 1)
            dve.memset(probs[:, 1, :, :], 0.0).then_inc(s_setup, 1)
            dve.memset(v[:, :, :, HD:VW], 1.0).then_inc(s_setup, 1)
            dve.wait_ge(s_w[0], 80)
            dve.tensor_scalar(bqs[:], colv[:, BQ:BQ + C], QSCALE, None, ALU.mult).then_inc(s_setup, 1)
            dve.wait_ge(s_w[1], 32)
            for c in range(XC):
                at = P * (c % 2)
                fold = dve.scalar_tensor_tensor(out=convw[:, c, at:at + P], in0=ident[:], scalar=0.5,
                                                in1=convw[:, c, at:at + P], op0=ALU.mult, op1=ALU.add)
            fold.then_inc(s_fold, 1)

            dve.sem_inc(s_hid, PRIME)
            dve.sem_inc(s_fd, PRIME)
            with dve.Fori(0, G) as g:
                def link(ins):
                    order[0] += 1
                    ins.then_inc(s_order, 1)
                    dve.wait_ge(s_order, g * LINKS + order[0])

                def layernorm(k, dst, last):
                    for j in range(T):
                        ins = dve.bn_stats(bst[:, j, :], h[:, j, :])
                    link(ins)
                    dve.memset(fence[:], 0.0)
                    for j in range(T):
                        ins = dve.bn_aggr(mv[:, j, :], bst[:, j, :])
                    ins.then_inc(s_var, 1)
                    dve.wait_ge(s_rstd, g * 3 + k + 1)
                    for j in range(T):
                        ins = dve.tensor_scalar(dst[:, j, :], h[:, j, :], mv[:, j, 0:1], rstd[:, j:j + 1],
                                                ALU.subtract, ALU.mult)
                        if last:
                            ins.then_inc(s_n, 1)
                    if not last:
                        link(ins)

                for c in range(1, XC, 2):
                    dve.wait_ge(s_xt_ps, g * XC + c + 1)
                    dve.tensor_copy(xT[:, c, :], ps[:, c, :]).then_inc(s_xt_v, 1)
                for j in range(T):
                    dve.wait_ge(s_conv, g * 4 + j + 1)
                    ins = dve.tensor_tensor(h[:, j, :], ps[:, 4 + j, 0:D], rowv[:, CONV_B, :], ALU.add)
                link(ins)
                layernorm(0, h, False)
                link(dve.tensor_tensor(h[:], h[:], rowv[:, GAMMA:GAMMA + 1, :].broadcast_to([P, T, D]), ALU.mult))
                link(dve.tensor_tensor(h[:], h[:], rowv[:, BETA:BETA + 1, :].broadcast_to([P, T, D]), ALU.add))
                layernorm(1, n, True)

                for a in range(2):
                    dve.wait_ge(s_nT_ps, g * 4 + 2 * a + 2)
                    dve.tensor_copy(nT[:, 1, :], ps[:, 1, :]).then_inc(s_nT_v, 1)
                    for c in range(C):
                        dve.wait_ge(s_qk_ps, g * 8 + 4 * a + 2 + c + 1)
                        for e in range(2):
                            m = colv[:, MEVEN + e:MEVEN + e + 1]
                            if a == 0:
                                ins = dve.tensor_scalar(kT[:, c, e, :], ps[:, 4 + c, :], colv[:, BK + c:BK + c + 1], m,
                                                        ALU.add, ALU.mult)
                            else:
                                ins = dve.tensor_scalar(kT[:, c, e, :], ps[:, 4 + c, :], m, None, ALU.mult)
                        ins.then_inc(s_k, 1)
                    if a == 0:
                        for j in range(T):
                            dve.wait_ge(s_v_ps, g * 8 + j + 1)
                            dve.tensor_tensor(v[:, j, :, 0:HD], ps[:, (6 + j) % 8, 0:D].rearrange("p (h d) -> p h d", d=HD),
                                              rowv[:, BV, :].rearrange("p (h d) -> p h d", d=HD), ALU.add).then_inc(s_v0, 1)

                    def before(j):
                        k = 4 * a + j
                        dve.wait_ge(s_s_ps, g * 8 + k + 1)
                        if k >= 2:
                            dve.wait_ge(s_p, g * 16 + 2 * (k - 1))
                        sc = scores[:, j % 2, :, :]
                        dve.tensor_tensor(sc.rearrange("p (r q) k -> p r q k", r=4),
                                          ps[:, 0:4, 0:4 * SLOT].rearrange("p r (q k) -> p r q k", q=4),
                                          mask[:, :].unsqueeze(1).unsqueeze(1).broadcast_to([P, 4, 4, SLOT]),
                                          ALU.add).then_inc(s_s_read, 1)
                        dve.wait_ge(s_s_read, g * 8 + k + 1)
                        link(dve.tensor_reduce(mx[:], sc, AX, ALU.max))
                        dve.tensor_tensor(sc, sc, mx[:].unsqueeze(2).broadcast_to([P, H, SLOT]), ALU.subtract)\
                           .then_inc(s_s_sub, 1)

                    def after(j):
                        k = 4 * a + j
                        dve.wait_ge(s_pv, g * 32 + 4 * k + 4)
                        ov = ps[:, 6, 0:H * VW].rearrange("p (h d) -> p h d", d=VW)
                        link(dve.reciprocal(rinv[:], ov[:, :, HD]))
                        dve.tensor_tensor(o[:, j, :].rearrange("p (h d) -> p h d", d=HD), ov[:, :, 0:HD],
                                          rinv[:].unsqueeze(2).broadcast_to([P, H, HD]), ALU.mult).then_inc(s_o, 1)

                    before(0)
                    for j in range(T):
                        if j + 1 < T:
                            before(j + 1)
                        if a == 1 and j == 0:
                            dve.wait_ge(s_lg_ps, g + 1)
                            lp = ps[:, 7, 0:T * E].rearrange("p (j e) -> p j e", e=E)
                            link(dve.tensor_reduce(rs[:], lp, AX, ALU.max))
                            dve.tensor_tensor(lg[:], lp, rs[:].unsqueeze(2).broadcast_to([P, T, E]), ALU.subtract)\
                               .then_inc(s_lgs, 1)
                        if a == 1 and j == 2:
                            dve.wait_ge(s_lge, g + 1)
                            link(dve.tensor_reduce(rs[:], lg[:], AX, ALU.add))
                            link(dve.reciprocal(rs[:], rs[:]))
                            link(dve.tensor_tensor(pr[:], lg[:], rs[:].unsqueeze(2).broadcast_to([P, T, E]), ALU.mult))
                            other = pr[:].unsqueeze(2).broadcast_to([P, T, E, E])
                            own = pr[:].unsqueeze(3).broadcast_to([P, T, E, E])
                            g4 = gt[:].rearrange("p (j e) f -> p j e f", e=E)
                            e4 = eq[:].rearrange("p (j e) f -> p j e f", e=E)
                            dve.tensor_tensor(g4, other, own, ALU.is_gt)
                            link(dve.tensor_tensor(e4, other, own, ALU.is_equal))
                            low = lower[:].unsqueeze(1).broadcast_to([P, T, E * E])
                            ev = eq[:].rearrange("p (j e) f -> p j (e f)", e=E)
                            link(dve.tensor_tensor(ev, ev, low, ALU.mult))
                            link(dve.tensor_tensor(gt[:], gt[:], eq[:], ALU.add))
                            link(dve.tensor_reduce(rank[:].rearrange("p j e -> p (j e)"), gt[:], AX, ALU.add))
                            link(dve.scalar_tensor_tensor(out=cw[:], in0=rank[:], scalar=1.5, in1=pr[:],
                                                          op0=ALU.is_lt, op1=ALU.mult))
                        after(j)
                    dve.wait_ge(s_oT_ps, g * 4 + 2 * a + 2)
                    dve.tensor_copy(oT[:, 1, :], ps[:, 1, :]).then_inc(s_oT_v, 1)
                    if a == 0:
                        dve.wait_ge(s_hbo, g + 1)
                        for j in range(T):
                            dve.wait_ge(s_wo, g * 8 + j + 1)
                            ins = dve.tensor_tensor(h[:, j, :], ps[:, 4 + j, 0:D], h[:, j, :], ALU.add)
                        link(ins)
                        layernorm(2, n, True)

                dve.wait_ge(s_rms, g * 3 + 1)
                for j in range(T):
                    ins = dve.scalar_tensor_tensor(out=hd[:, j, :], in0=ps[:, 4 + j, 0:D], scalar=rms[:, ATT, j:j + 1],
                                                   in1=rowv[:, W_ATT, :], op0=ALU.mult, op1=ALU.mult)
                link(ins)
                dve.tensor_tensor(hd[:], hd[:], n[:], ALU.add).then_inc(s_hd, 1)

                def hidden(i):
                    dve.wait_ge(s_gate, g * U + i + 1)
                    if i < 4:
                        dve.wait_ge(s_down, PRIME + g * DOWNS)
                    else:
                        dve.wait_ge(s_down, PRIME + g * DOWNS + ((i - 4) // 2 + 1 if i - 4 < UE else E + i - 4 - UE + 1))
                    link(dve.scalar_tensor_tensor(out=up[:, i % 2, :], in0=gate[:, i % 2, :], scalar=1.0,
                                                  in1=ps[:, 2 * (i % 2), :], op0=ALU.add, op1=ALU.mult))
                    dve.scalar_tensor_tensor(out=hidT[:, i % 4, :], in0=up[:, i % 2, :], scalar=0.5,
                                             in1=ps[:, 2 * (i % 2) + 1, :], op0=ALU.mult, op1=ALU.mult).then_inc(s_hid, 1)

                def collect(e):
                    dve.wait_ge(s_down, PRIME + g * DOWNS + e + 1)
                    if e:
                        dve.wait_ge(s_moe, g * E + e)
                    for j in range(T):
                        src = ps[:, 4 + 2 * (e % 2) + j // 2, D * (j % 2):D * (j % 2) + D]
                        if e == 0:
                            ins = dve.tensor_scalar(moe[:, j, :], src, cw[:, j, e:e + 1], None, ALU.mult)
                        else:
                            ins = dve.scalar_tensor_tensor(out=moe[:, j, :], in0=src, scalar=cw[:, j, e:e + 1],
                                                           in1=moe[:, j, :], op0=ALU.mult, op1=ALU.add)
                    ins.then_inc(s_moe, 1)

                hidden(0)
                for e in range(E):
                    hidden(2 * e + 1)
                    if e < E - 1:
                        hidden(2 * e + 2)
                        collect(e)
                dve.wait_ge(s_hdT_ps, g * 2 + 2)
                dve.tensor_copy(hdT[:, 1, :], ps[:, 1, :]).then_inc(s_hdT_v, 1)
                collect(E - 1)
                for i in range(UE, U):
                    hidden(i)
                dve.wait_ge(s_out, PRIME + g * 32)
                link(dve.tensor_tensor(y[:], h[:], hd[:], ALU.add))
                for at, k, vec in ((MOE, 1, W_MOE), (DENSE, 2, W_FF)):
                    dve.wait_ge(s_rms, g * 3 + k + 1)
                    for j in range(T):
                        src = moe[:, j, :] if at == MOE else ps[:, 4 + j, 0:D]
                        ins = dve.scalar_tensor_tensor(out=o[:, j, :], in0=src, scalar=rms[:, at, j:j + 1],
                                                       in1=rowv[:, vec, :], op0=ALU.mult, op1=ALU.mult)
                        if at == DENSE:
                            ins.then_inc(s_fd, 1)
                    if at == MOE:
                        link(ins)
                        link(dve.tensor_tensor(y[:], y[:], o[:], ALU.add))
                    else:
                        dve.wait_ge(s_fd, PRIME + g * T + T)
                        dve.tensor_tensor(y[:], y[:], o[:], ALU.add).then_inc(s_y, 1)
            assert order[0] == LINKS


def kernel(x, L0_tok_conv_w, L0_tok_conv_b, L0_tok_ln_gamma, L0_tok_ln_beta, L0_attn_Wq, L0_attn_bq, L0_attn_Wk,
           L0_attn_bk, L0_attn_Wv, L0_attn_bv, L0_attn_Wo, L0_attn_bo, L0_ffn_wq, L0_ffn_wk, L0_ffn_wv, L0_ffn_wo,
           L0_ffn_w1, L0_ffn_w2, L0_ffn_w3, L0_ffn_attn_norm_w, L0_ffn_ff_norm_w, L0_ffn_moe_norm_w, L0_ffn_router_w,
           L0_ffn_ew1, L0_ffn_ew2, L0_ffn_ew3):
    import numpy as np
    import concourse.bacc as bacc
    from concourse.bass_utils import run_bass_kernel_spmd

    def contraction_first(w):
        w = np.asarray(w)
        w = w.reshape(w.shape[:-2] + (w.shape[-2] // P, P, w.shape[-1]))
        return np.ascontiguousarray(np.moveaxis(w, -2, 0))

    def per_feature(b):
        return np.asarray(b).reshape(C, P).T

    rows = np.stack([np.asarray(b) for b in (L0_tok_conv_b, L0_tok_ln_gamma, L0_tok_ln_beta, L0_attn_bv, L0_attn_bo,
                                             L0_ffn_attn_norm_w, L0_ffn_ff_norm_w, L0_ffn_moe_norm_w)])
    even = (np.arange(P) % 32 < HD).astype(np.float32)[:, None]
    row = np.arange(P)[:, None] % SLOT
    arrays = {
        "x": np.asarray(x).reshape(G, T, 2, L, D),
        "rows": np.ascontiguousarray(np.broadcast_to(rows, (P,) + rows.shape)),
        "cols": np.concatenate([per_feature(L0_attn_bq), per_feature(L0_attn_bk), even, 1 - even], axis=1),
        "ident": np.eye(P, dtype=np.float32),
        "mask": np.where(np.arange(SLOT)[None, :] <= row, 0.0, NEG).astype(np.float32),
        "lower": np.ascontiguousarray(np.broadcast_to(np.tril(np.ones((E, E), np.float32), -1).reshape(1, -1), (P, E * E))),
        "conv_w": contraction_first(np.asarray(L0_tok_conv_w).transpose(2, 1, 0).reshape(2 * D, D)),
        "attn_w": contraction_first(np.stack([np.asarray(w).T for w in (L0_attn_Wq, L0_attn_Wk, L0_attn_Wv, L0_attn_Wo)]
                                             + [np.asarray(w) for w in (L0_ffn_wq, L0_ffn_wk, L0_ffn_wv, L0_ffn_wo)])),
        "w1": contraction_first(L0_ffn_w1),
        "w3": contraction_first(L0_ffn_w3),
        "w2": contraction_first(L0_ffn_w2),
        "router": contraction_first(L0_ffn_router_w),
        "ew1": contraction_first(L0_ffn_ew1),
        "ew3": contraction_first(L0_ffn_ew3),
        "ew2": contraction_first(L0_ffn_ew2),
    }
    nc = bacc.Bacc("TRN2", target_bir_lowering=False, num_devices=1)
    arrays = {f"in_{k}": np.ascontiguousarray(a) for k, a in arrays.items()}
    aps = [nc.dram_tensor(k, a.shape, F32, kind="ExternalInput").ap() for k, a in arrays.items()]
    out = nc.dram_tensor("out", (G, T, 2, TOK, D), F32, kind="ExternalOutput").ap()
    program(nc, *aps, out)
    r = run_bass_kernel_spmd(nc, [arrays], core_ids=[0])
    return r.results[0]["out"].reshape(B, TOK, D)
```

```python
from contextlib import ExitStack

import concourse.bass as bass
from concourse import mybir

F32 = mybir.dt.float32
F32R = mybir.dt.float32r
ACT = mybir.ActivationFunctionType
ALU = mybir.AluOpType
AX = mybir.AxisListType.X

P = 128
B, L, D = 64, 125, 256
TOK = (L + 1) // 2
SLOT = 64
T = 4
G = B // (2 * T)
C = D // P
GT = T * P
H, HD = 16, 16
R = 4
VW = HD + 1
FF, E = 1024, 8
UD = FF // P
UE = E * D // P
XC = 2 * D // P
EPS = 1e-5
NEG = -1e30
QSCALE = HD ** -0.5
LINKS_A, LINKS_B = 17, 23
PRIME = 1

CONV_B, GAMMA, BETA, BV, BO, W_ATT, W_FF, W_MOE = range(8)
BQ, BK, MEVEN, MODD, PAIR = 0, 2, 4, 5, 6


def program(nc, x, rows, cols, ident_in, mask_in, lower_in, conv_w, attn_w, w1_in, w3_in, w2_in, router_in,
            ew1_in, ew3_in, ew2_in, out):
    ctx = ExitStack()
    with ctx:
        def dram(name, shape):
            return nc.dram_tensor(name, shape, F32, kind="Internal").ap()

        def sem(name):
            return ctx.enter_context(nc.semaphore(name))

        y_mid = dram("y_mid", (G, P, T * D))
        n_mid = dram("n_mid", (G, P, C * GT))
        c_mid = dram("c_mid", (G, P, T * E))

        def sb(name, shape, dt=F32):
            return ctx.enter_context(nc.sbuf_tensor(name, shape, dt))

        rowv = sb("rowv", [P, 8, D])
        nhalf = sb("nhalf", [P, T])
        epsv = sb("epsv", [P, T])

        first = ExitStack()

        def s1(name, shape):
            return first.enter_context(nc.sbuf_tensor(name, shape, F32))

        convw = s1("convw", [P, XC, D])
        attnw = s1("attnw", [P, 8, C, D])
        w1 = s1("w1", [P, C, FF])
        w3 = s1("w3", [P, C, FF])
        w2 = s1("w2", [P, UD, D])
        router = s1("router", [P, C, E])
        colv = s1("colv", [P, 6 + R])
        qscale = s1("qscale", [P, 2])
        qbias = s1("qbias", [P, C, 2])
        ident = s1("ident", [P, P])
        identr = first.enter_context(nc.sbuf_tensor("identr", [P, P], F32R))
        maskr = first.enter_context(nc.sbuf_tensor("maskr", [P, C * R // 2, SLOT], F32R))
        mask = s1("mask", [P, SLOT])
        lower = s1("lower", [P, E * E])
        x_in = s1("x_in", [P, T, 2 * D])
        xT = s1("xT", [P, XC, GT])
        h0 = s1("h0", [P, T, D])
        h = s1("h", [P, T, D])
        n = [s1(f"n{a}", [P, T, D]) for a in range(2)]
        nT = s1("nT", [P, C, GT])
        qE = [s1(f"qE{a}", [P, C, 2 * T, 2, SLOT]) for a in range(2)]
        kT = [s1(f"kT{a}", [P, T, C, P]) for a in range(2)]
        kM = s1("kM", [P, 2, C, 2, R, SLOT])
        v = [s1(f"v{a}", [P, T, H, 2, VW]) for a in range(2)]
        scores = s1("scores", [P, C * R, 2, SLOT])
        probs = s1("probs", [P, C * R, 2, SLOT])
        pT = s1("pT", [P, C, R * P])
        o = s1("o", [P, T, 2, P])
        oT = s1("oT", [P, 2, GT])
        rt = s1("rt", [P, T, D])
        hd = s1("hd", [P, T, D])
        hdT = s1("hdT", [P, C, GT])
        gate = s1("gate", [P, 2, GT])
        up = s1("up", [P, GT])
        hidT = s1("hidT", [P, 4, GT])
        y = s1("y", [P, T, D])
        junk = s1("junk", [P, 2 * T, D])
        bst = s1("bst", [P, T, 6])
        mv = s1("mv", [P, T, 2])
        vare = s1("vare", [P, T])
        rstd = s1("rstd", [P, T])
        fence = s1("fence", [P, 1])
        ss = s1("ss", [P, 2, T])
        msq = s1("msq", [P, 2, T])
        rms = s1("rms", [P, 2, T])
        mx = s1("mx", [P, H])
        rinv = s1("rinv", [P, H])
        lg = s1("lg", [P, T, E])
        pr = s1("pr", [P, T, E])
        rs = s1("rs", [P, T])
        gt = s1("gt", [P, T * E, E])
        eq = s1("eq", [P, T * E, E])
        rank = s1("rank", [P, T, E])
        cw = s1("cw", [P, T, E])
        first.close()

        def s2(name, shape, dt=F32):
            return sb(name, shape, dt)

        wh = s2("wh", [P, E, 3, C, D], F32R)
        wl = s2("wl", [P, E, 3, C, D], F32R)
        raw = s2("raw", [P, 2, 3, C, D])
        m_in = s2("m_in", [P, C, GT])
        mh = s2("mh", [P, C, GT], F32R)
        ml = s2("ml", [P, C, GT], F32R)
        mgate = s2("mgate", [P, 2, GT])
        mup = s2("mup", [P, GT])
        mhid = s2("mhid", [P, 2, GT])
        hh = s2("hh", [P, 4, GT], F32R)
        hl = s2("hl", [P, 4, GT], F32R)
        mcw = s2("mcw", [P, T, E])
        moe = s2("moe", [P, T, D])
        moe2 = s2("moe2", [P, T, D])
        my = s2("my", [P, T, D])
        mjunk = s2("mjunk", [P, T, D])
        mss = s2("mss", [P, T])
        mms = s2("mms", [P, T])
        mrms = s2("mrms", [P, T])

        ps = ctx.enter_context(nc.psum_tensor("ps", [P, 8, 512], F32))

        s_w = [sem(f"s_w{i}") for i in range(4)]
        names = ("x pad const setup fold xt_ps xt_a xt_v conv order_a order_b var vare rstd n hbo nT_ps nT_a "
                 "q_ps k_ps q k km v_ps v0 v1 s_ps s_sub p pT_ps pT_a pv o oT_ps oT_a wo ss msq rms rt "
                 "hd hdT_ps hdT_a up_ps gate hid down y0 y1 y yst nst cst lg_ps lgs lge cw "
                 "end_pe end_act end_dve end_pool wh wl m_in my_in mh ml mup_ps mgate mu mhid mhh mhl mdown moe "
                 "mss mms mrms mt my out").split()
        sems = {name: sem("s_" + name) for name in names}
        (s_x, s_pad, s_const, s_setup, s_fold, s_xt_ps, s_xt_a, s_xt_v, s_conv, s_order_a, s_order_b, s_var, s_vare,
         s_rstd, s_n, s_hbo, s_nT_ps, s_nT_a, s_q_ps, s_k_ps, s_q, s_k, s_km, s_v_ps, s_v0, s_v1, s_s_ps,
         s_s_sub, s_p, s_pT_ps, s_pT_a, s_pv, s_o, s_oT_ps, s_oT_a, s_wo, s_ss, s_msq, s_rms, s_rt,
         s_hd, s_hdT_ps, s_hdT_a, s_up_ps, s_gate, s_hid, s_down, s_y0, s_y1, s_y, s_yst, s_nst, s_cst,
         s_lg_ps, s_lgs, s_lge, s_cw, s_end_pe, s_end_act, s_end_dve, s_end_pool, s_wh, s_wl, s_m_in, s_my_in,
         s_mh, s_ml, s_mup_ps, s_mgate, s_mu, s_mhid, s_mhh, s_mhl, s_mdown, s_moe, s_mss, s_mms, s_mrms, s_mt, s_my,
         s_out) = (sems[name] for name in names)

        s_raw = [sem(f"s_raw{i}") for i in range(2)]

        block = ctx.enter_context(nc.Block())

        def head(c, r, e):
            return 8 * c + 2 * r + e

        def past(eng, s, value):
            if not (isinstance(value, int) and value <= 0):
                eng.wait_ge(s, value)

        def pipeline(eng, half):
            half(0, None)
            with eng.Fori(0, G - 1) as g:
                half(g + 1, g)
            half(None, G - 1)

        @block.sync
        def _(sp):
            def load_x(g):
                for s in range(2):
                    src = x[g, :, s]
                    sp.dma_start(x_in[SLOT * s:SLOT * s + TOK - 1, :, :],
                                 src[:, 0:L - 1, :].rearrange("j (t k) i -> t j (k i)", k=2)).then_inc(s_x, 16)
                    sp.dma_start(x_in[SLOT * s + TOK - 1:SLOT * s + TOK, :, 0:D],
                                 src[:, L - 1:L, :].rearrange("j t i -> t j i")).then_inc(s_x, 16)

            def save_a(g):
                sp.wait_ge(s_nT_a, g * 4 + 4)
                sp.dma_start(n_mid[g], nT[:, :, :].rearrange("p c r -> p (c r)")).then_inc(s_nst, 16)

            def save_b(g):
                sp.wait_ge(s_cw, g + 1)
                sp.dma_start(c_mid[g], cw[:, :, :].rearrange("p j e -> p (j e)")).then_inc(s_cst, 16)
                sp.wait_ge(s_y, g + 1)
                sp.dma_start(y_mid[g], y[:, :, :].rearrange("p j i -> p (j i)")).then_inc(s_yst, 16)

            sp.dma_start(ident[:], ident_in).then_inc(s_w[0], 16)
            sp.dma_start(mask[:], mask_in).then_inc(s_w[0], 16)
            sp.dma_start(lower[:], lower_in).then_inc(s_w[0], 16)
            sp.dma_start(colv[:], cols).then_inc(s_w[0], 16)
            sp.dma_start(rowv[:], rows).then_inc(s_w[0], 16)
            sp.sem_inc(s_yst, PRIME)
            sp.sem_inc(s_cst, PRIME)
            sp.wait_ge(s_pad, 2)
            load_x(0)
            sp.dma_start(convw[:], conv_w).then_inc(s_w[1], 16)
            sp.dma_start(attnw[:], attn_w).then_inc(s_w[2], 16)
            sp.dma_start(router[:], router_in).then_inc(s_w[2], 16)
            sp.dma_start(w1[:], w1_in).then_inc(s_w[3], 16)
            sp.dma_start(w3[:], w3_in).then_inc(s_w[3], 16)
            sp.dma_start(w2[:], w2_in).then_inc(s_w[3], 16)
            sp.wait_ge(s_xt_ps, XC)
            load_x(1)
            save_a(0)
            with sp.Fori(0, G - 2) as g:
                sp.wait_ge(s_xt_ps, g * XC + 2 * XC)
                load_x(g + 2)
                save_b(g)
                save_a(g + 1)
            save_b(G - 2)
            save_a(G - 1)
            save_b(G - 1)

            for s in (s_end_pe, s_end_act, s_end_dve, s_end_pool):
                sp.wait_ge(s, 1)
            sp.wait_ge(s_nst, G * 16)
            sp.wait_ge(s_cst, PRIME + G * 16)
            sp.wait_ge(s_yst, PRIME + G * 16)

            def load_m(g):
                sp.dma_start(m_in[:, :, :].rearrange("p c r -> p (c r)"), n_mid[g]).then_inc(s_m_in, 16)

            def load_w(e):
                for i, w in enumerate((ew1_in, ew3_in, ew2_in)):
                    sp.dma_start(raw[:, e % 2, i, :, :], w[:, e, :, :]).then_inc(s_raw[e % 2], 16)

            load_m(0)
            for e in range(E):
                if e >= 2:
                    sp.wait_ge(s_wl, e - 1)
                load_w(e)

            def load_rest(g):
                sp.wait_ge(s_out, PRIME + g * 32)
                sp.wait_ge(s_moe, PRIME + g * E)
                sp.dma_start(mcw[:, :, :].rearrange("p j e -> p (j e)"), c_mid[g]).then_inc(s_my_in, 16)
                sp.dma_start(my[:, :, :].rearrange("p j i -> p (j i)"), y_mid[g]).then_inc(s_my_in, 16)

            def store(g):
                sp.wait_ge(s_my, g + 1)
                for s in range(2):
                    sp.dma_start(out[g, :, s].rearrange("j t i -> t j i"),
                                 my[SLOT * s:SLOT * s + TOK, :, :]).then_inc(s_out, 16)

            sp.sem_inc(s_out, PRIME)
            with sp.Fori(0, G - 1) as g:
                load_rest(g)
                sp.wait_ge(s_mh, g + 1)
                sp.wait_ge(s_ml, g + 1)
                load_m(g + 1)
                store(g)
            load_rest(G - 1)
            store(G - 1)
            sp.wait_ge(s_out, PRIME + G * 32)

        @block.gpsimd
        def _(pool):
            pool.memset(x_in[:, 0:2, :], 0.0).then_inc(s_pad, 1)
            pool.memset(x_in[:, 2:4, :], 0.0).then_inc(s_pad, 1)
            pool.memset(nhalf[:], -0.5).then_inc(s_const, 1)
            pool.memset(epsv[:], EPS).then_inc(s_const, 1)
            pool.wait_ge(s_const, 2)
            pool.wait_ge(s_w[0], 80)

            def power(g, k):
                pool.wait_ge(s_var, g * 3 + k + 1)
                pool.tensor_tensor(vare[:], mv[:, :, 1], epsv[:], ALU.add).then_inc(s_vare, 1)
                pool.wait_ge(s_vare, g * 3 + k + 1)
                pool.tensor_tensor(rstd[:], vare[:], nhalf[:], ALU.pow).then_inc(s_rstd, 1)

            def rms_power(g, k):
                pool.wait_ge(s_ss, g * (2 * T) + T * (k + 1))
                pool.tensor_tensor(msq[:, k, :], ss[:, k, :], epsv[:], ALU.add).then_inc(s_msq, 1)
                pool.wait_ge(s_msq, g * 2 + k + 1)
                pool.tensor_tensor(rms[:, k, :], msq[:, k, :], nhalf[:], ALU.pow).then_inc(s_rms, 1)

            def mask_keys(a, g, j):
                k = 4 * a + j
                if j == 0:
                    pool.wait_ge(s_k, g * 4 + 2 * a + 2)
                past(pool, s_s_ps, g * 8 + k - 1)
                src = kT[a][:, j, :, :].rearrange("p c (s k) -> p (c s) k", s=2).unsqueeze(2).broadcast_to([P, 2 * C, R, SLOT])
                own = colv[:, PAIR:PAIR + R].unsqueeze(1).unsqueeze(3).broadcast_to([P, 2 * C, R, SLOT])
                pool.tensor_tensor(kM[:, j % 2, :, :, :, :].rearrange("p c s r k -> p (c s) r k"), src, own, ALU.mult)\
                    .then_inc(s_km, 1)

            def half(ga, gb):
                if gb is not None:
                    mask_keys(1, gb, 0)
                    mask_keys(1, gb, 1)
                    pool.wait_ge(s_yst, PRIME + gb * 16)
                    pool.tensor_tensor(y[:], h[:], n[1][:], ALU.add).then_inc(s_y0, 1)
                if ga is not None:
                    power(ga, 0)
                if gb is not None:
                    mask_keys(1, gb, 2)
                if ga is not None:
                    power(ga, 1)
                if gb is not None:
                    mask_keys(1, gb, 3)
                    rms_power(gb, 0)
                if ga is not None:
                    mask_keys(0, ga, 0)
                    mask_keys(0, ga, 1)
                if gb is not None:
                    pool.wait_ge(s_y0, gb + 1)
                    pool.wait_ge(s_rt, PRIME + gb * 2 + 1)
                    pool.tensor_tensor(y[:], y[:], rt[:], ALU.add).then_inc(s_y1, 1)
                if ga is not None:
                    pool.wait_ge(s_n, ga * (2 * T) + T)
                    pool.tensor_tensor(h0[:], h0[:], rowv[:, BO:BO + 1, :].broadcast_to([P, T, D]), ALU.add)\
                        .then_inc(s_hbo, 1)
                    mask_keys(0, ga, 2)
                    mask_keys(0, ga, 3)
                    power(ga, 2)
                if gb is not None:
                    rms_power(gb, 1)
                    pool.wait_ge(s_y1, gb + 1)
                    pool.wait_ge(s_rt, PRIME + gb * 2 + 2)
                    pool.tensor_tensor(y[:], y[:], rt[:], ALU.add).then_inc(s_y, 1)

            pipeline(pool, half)
            pool.wait_ge(s_y, G)
            pool.memset(msq[:, 0, :], 0.0).then_inc(s_end_pool, 1)

            with pool.Fori(0, G) as g:
                for i in range(UE):
                    pool.wait_ge(s_mhh, g * UE + i + 1)
                    pool.wait_ge(s_mdown, PRIME + g * E + (i // 2 - 1 if i >= 4 else 0))
                    pool.tensor_tensor(hl[:, i % 4, :], mhid[:, i % 2, :], hh[:, i % 4, :].bitcast(F32), ALU.subtract)\
                        .then_inc(s_mhl, 1)
                pool.wait_ge(s_mss, g * T + T)
                pool.tensor_tensor(mms[:], mss[:], epsv[:], ALU.add).then_inc(s_mms, 1)
                pool.wait_ge(s_mms, g + 1)
                pool.tensor_tensor(mrms[:], mms[:], nhalf[:], ALU.pow).then_inc(s_mrms, 1)

        @block.scalar
        def _(act):
            act.wait_ge(s_w[0], 80)
            act.wait_ge(s_setup, 8)

            def exps(a, g, j):
                act.wait_ge(s_s_sub, g * 8 + 4 * a + j + 1)
                act.activation(probs[:], scores[:], ACT.Exp).then_inc(s_p, 1)

            def evac(a, g, j):
                k = 4 * a + j
                for c in range(C):
                    act.wait_ge(s_pT_ps, g * 16 + 2 * k + c + 1)
                    past(act, s_pv, g * 16 + 2 * k + c - 1)
                    act.activation(pT[:, c, :], ps[:, 2, :], ACT.Copy).then_inc(s_pT_a, 1)

            def evac_n(a, g):
                past(act, s_nst, g * 16)
                bank = 0 if a else 4
                for c in range(C):
                    act.wait_ge(s_nT_ps, g * 4 + 2 * a + c + 1)
                    act.activation(nT[:, c, :], ps[:, bank + c, :], ACT.Copy).then_inc(s_nT_a, 1)

            def evac_q(a, g):
                bank = 0 if a else 6
                for c in range(C):
                    act.wait_ge(s_q_ps, g * 4 + 2 * a + c + 1)
                    src = ps[:, bank + c, :].rearrange("p (t q) -> p t q", q=SLOT)
                    for e in range(2):
                        ins = act.activation(qE[a][:, c, :, e, :], src, ACT.Identity, scale=qscale[:, e:e + 1],
                                             bias=0.0 if a else qbias[:, c, e:e + 1])
                    ins.then_inc(s_q, 1)

            def evac_o(a, g):
                for b in range(2):
                    act.wait_ge(s_oT_ps, g * 4 + 2 * a + b + 1)
                    act.activation(oT[:, :, 2 * P * b:2 * P * (b + 1)].rearrange("p e (t q) -> p t e q", q=SLOT),
                                   ps[:, b, :].rearrange("p (t e q) -> p t e q", e=2, q=SLOT), ACT.Copy).then_inc(s_oT_a, 1)

            def gates(g, i):
                act.wait_ge(s_up_ps, g * UD + i + 1)
                if i >= 2:
                    act.wait_ge(s_hid, g * UD + i - 1)
                act.activation(gate[:, i % 2, :], ps[:, 4, :], ACT.Tanh, scale=0.5).then_inc(s_gate, 1)

            def squares(g, k):
                for j in range(T):
                    if k == 0:
                        act.wait_ge(s_wo, g * 4 + 2 + j // 2 + 1)
                        src = ps[:, 2 + j // 2, D * (j % 2):D * (j % 2) + D]
                    else:
                        act.wait_ge(s_down, g * UD + UD)
                        src = ps[:, 6 + j // 2, D * (j % 2):D * (j % 2) + D]
                    act.activation(junk[:, T * k + j, :], src, ACT.Square, scale=D ** -0.5,
                                   accum_out=ss[:, k, j:j + 1]).then_inc(s_ss, 1)

            def half(ga, gb):
                A, Bh = ga is not None, gb is not None
                if A:
                    for c in range(0, XC, 2):
                        act.wait_ge(s_xt_ps, ga * XC + c + 1)
                        act.activation(xT[:, c, :], ps[:, 4 + c, :], ACT.Copy).then_inc(s_xt_a, 1)
                if Bh:
                    for j in range(2):
                        exps(1, gb, j)
                        evac(1, gb, j)
                    exps(1, gb, 2)
                if A:
                    evac_n(0, ga)
                if Bh:
                    evac(1, gb, 2)
                    exps(1, gb, 3)
                    evac(1, gb, 3)
                if A:
                    evac_q(0, ga)
                if Bh:
                    evac_o(1, gb)
                    squares(gb, 0)
                    for c in range(C):
                        act.wait_ge(s_hdT_ps, gb * 2 + c + 1)
                        act.activation(hdT[:, c, :], ps[:, 4 + c, :], ACT.Copy).then_inc(s_hdT_a, 1)
                if A:
                    exps(0, ga, 0)
                if Bh:
                    gates(gb, 0)
                for j in range(T):
                    if A:
                        evac(0, ga, j)
                        if j + 1 < T:
                            exps(0, ga, j + 1)
                    if Bh:
                        gates(gb, j + 1)
                if A:
                    evac_o(0, ga)
                if Bh:
                    gates(gb, 5)
                    gates(gb, 6)
                if A:
                    evac_n(1, ga)
                if Bh:
                    gates(gb, 7)
                    squares(gb, 1)
                if A:
                    evac_q(1, ga)
                    for b in range(2):
                        act.wait_ge(s_v_ps, ga * 4 + 2 + b + 1)
                        for s in range(2):
                            rows = slice(SLOT * s, SLOT * s + SLOT)
                            act.activation(v[1][rows, 2 * b:2 * b + 2, :, s, 0:HD].rearrange("p j h d -> p (j h) d"),
                                           ps[rows, 2 + b, :].rearrange("p (h d) -> p h d", d=HD), ACT.Copy)\
                                .then_inc(s_v1, 1)
                    act.wait_ge(s_lgs, ga + 1)
                    act.activation(lg[:], lg[:], ACT.Exp).then_inc(s_lge, 1)

            pipeline(act, half)
            act.wait_ge(s_ss, G * 2 * T)
            act.activation(junk[:, 0, 0:T], nhalf[:], ACT.Copy).then_inc(s_end_act, 1)

            act.wait_ge(s_end_pe, 1)
            act.wait_ge(s_end_dve, 1)
            act.wait_ge(s_end_pool, 1)
            for e in range(E):
                act.wait_ge(s_raw[e % 2], 48 * (e // 2 + 1))
                act.activation(wh[:, e, :, :, :], raw[:, e % 2, :, :, :], ACT.Copy).then_inc(s_wh, 1)
            with act.Fori(0, G) as g:
                act.wait_ge(s_m_in, g * 16 + 16)
                act.wait_ge(s_mdown, PRIME + g * E)
                act.activation(mh[:], m_in[:], ACT.Copy).then_inc(s_mh, 1)
                for i in range(UE + 1):
                    if i < UE:
                        act.wait_ge(s_mup_ps, g * UE + i + 1)
                        if i >= 2:
                            act.wait_ge(s_mu, g * UE + i - 1)
                        act.activation(mgate[:, i % 2, :], ps[:, 2 * (i % 2), :], ACT.Tanh, scale=0.5).then_inc(s_mgate, 1)
                    if i >= 1:
                        k = i - 1
                        act.wait_ge(s_mhid, PRIME + g * UE + k + 1)
                        if k >= 4:
                            act.wait_ge(s_mdown, PRIME + g * E + k // 2 - 1)
                        act.activation(hh[:, k % 4, :], mhid[:, k % 2, :], ACT.Copy).then_inc(s_mhh, 1)
                act.wait_ge(s_moe, PRIME + g * E + E)
                for j in range(T):
                    act.activation(mjunk[:, j, :], moe[:, j, :], ACT.Square, scale=D ** -0.5,
                                   accum_out=mss[:, j:j + 1]).then_inc(s_mss, 1)

        @block.tensor
        def _(pe):
            pe.wait_ge(s_w[0], 80)
            pe.wait_ge(s_setup, 8)

            def project(dst, left, right, chunks=C):
                for c in range(chunks):
                    mm = pe.matmul(dst, left(c), right(c), start=(c == 0), stop=(c == chunks - 1))
                return mm

            def turn(src, bank, done, chunks=C):
                for c in range(chunks):
                    for j in range(T):
                        mm = pe.transpose(ps[:, bank + c, P * j:P * j + P], src[:, j, P * c:P * c + P], ident[:])
                    mm.then_inc(done, 1)

            def turn_x(g):
                pe.wait_ge(s_x, g * 64 + 64)
                if not isinstance(g, int):
                    pe.wait_ge(s_k, g * 4)
                    pe.wait_ge(s_lgs, g)
                if not isinstance(g, int):
                    pe.wait_ge(s_rt, PRIME + (g - 1) * 2)
                turn(x_in, 4, s_xt_ps, XC)

            def conv(g):
                if isinstance(g, int):
                    pe.wait_ge(s_fold, 1)
                pe.wait_ge(s_xt_a, g * 2 + 2)
                pe.wait_ge(s_xt_v, g * 2 + 2)
                for j in range(T):
                    project(ps[:, 4 + j, 0:D], lambda c: xT[:, c, P * j:P * j + P], lambda c: convw[:, c, :], XC)\
                        .then_inc(s_conv, 1)

            def turn_n(a, g):
                pe.wait_ge(s_n, g * (2 * T) + T * (a + 1))
                if a:
                    pe.wait_ge(s_oT_a, g * 4 + 2)
                turn(n[a], 0 if a else 4, s_nT_ps)

            def queries(a, g):
                pe.wait_ge(s_nT_a, g * 4 + 2 * a + 2)
                if a == 0 and isinstance(g, int):
                    pe.wait_ge(s_w[2], 32)
                for c in range(C):
                    project(ps[:, (0 if a else 6) + c, :], lambda k: attnw[:, 4 * a, k, P * c:P * c + P],
                            lambda k: nT[:, k, :]).then_inc(s_q_ps, 1)

            def keys(a, g):
                for c in range(C):
                    project(ps[:, 4 + c, :], lambda k: attnw[:, 4 * a + 1, k, P * c:P * c + P],
                            lambda k: nT[:, k, :]).then_inc(s_k_ps, 1)

            def values(a, g):
                if a == 0:
                    pe.wait_ge(s_q, g * 4 + 2)
                for j in range(T):
                    bank = (2 if a else 6) + j // 2
                    mm = project(ps[:, bank, D * (j % 2):D * (j % 2) + D], lambda k: nT[:, k, P * j:P * j + P],
                                 lambda k: attnw[:, 4 * a + 2, k, :])
                    if j % 2:
                        mm.then_inc(s_v_ps, 1)

            def score(a, g, j):
                k = 4 * a + j
                if j == 0:
                    if a == 0:
                        past(pe, s_oT_a, g * 4)
                    else:
                        pe.wait_ge(s_q, g * 4 + 4)
                else:
                    pe.wait_ge(s_s_sub, g * 8 + k)
                for s in range(2):
                    for c in range(C):
                        pe.matmul(ps[:, s, R * SLOT * c:R * SLOT * (c + 1)], identr[:], maskr[:], start=(c == 0),
                                  stop=False, skip_group_check=True)
                pe.wait_ge(s_km, g * 8 + k + 1)
                if j == 0 and a == 0:
                    pe.wait_ge(s_q, g * 4 + 2)
                for s in range(2):
                    for c in range(C):
                        mm = pe.matmul(ps[:, s, R * SLOT * c:R * SLOT * (c + 1)], qE[a][:, c, 2 * j + s, :, :],
                                       kM[:, j % 2, c, s, :, :], start=False, stop=True, skip_group_check=True)
                mm.then_inc(s_s_ps, 1)

            def turn_p(a, g, j, c):
                k = 4 * a + j
                if c == 0:
                    pe.wait_ge(s_p, g * 8 + k + 1)
                    if j == 0 and a == 0:
                        past(pe, s_hd, g)
                    if j == 0 and a == 1:
                        pe.wait_ge(s_v1, g * 4 + 4)
                    if j > 0:
                        pe.wait_ge(s_pT_a, g * 16 + 2 * k)
                else:
                    pe.wait_ge(s_pT_a, g * 16 + 2 * k + 1)
                for r in range(R):
                    mm = pe.transpose(ps[:, 2, P * r:P * r + P], probs[:, R * c + r, :, :], ident[:])
                mm.then_inc(s_pT_ps, 1)

            def weigh(a, g, j, c):
                k = 4 * a + j
                pe.wait_ge(s_pT_a, g * 16 + 2 * k + c + 1)
                if c == 0 and j == 0:
                    pe.wait_ge(s_v1 if a else s_v0, g * 4 + 4)
                if c == 0 and j > 0:
                    pe.wait_ge(s_o, g * 8 + k)
                for r in range(R):
                    for e in range(2):
                        at = 2 * VW * (R * c + r)
                        mm = pe.matmul(ps[SLOT * e:SLOT * e + SLOT, 3, at:at + 2 * VW],
                                       pT[:, c, P * r + SLOT * e:P * r + SLOT * e + SLOT], v[a][:, j, head(c, r, e), :, :],
                                       start=True, stop=True)
                mm.then_inc(s_pv, 1)

            def turn_o(a, g):
                pe.wait_ge(s_o, g * 8 + 4 * a + 4)
                for b in range(2):
                    for t in range(4):
                        mm = pe.transpose(ps[:, b, P * t:P * t + P], o[:, 2 * b + t // 2, t % 2, :], ident[:])
                    mm.then_inc(s_oT_ps, 1)

            def project_o(a, g):
                pe.wait_ge(s_oT_a, g * 4 + 2 * a + 2)
                for j in range(T):
                    mm = project(ps[:, 2 + j // 2, D * (j % 2):D * (j % 2) + D], lambda e: oT[:, e, P * j:P * j + P],
                                 lambda e: attnw[:, 4 * a + 3, e, :])
                    if j % 2:
                        mm.then_inc(s_wo, 1)

            def ups(g, i):
                if i == 0:
                    pe.wait_ge(s_hdT_a, g * 2 + 2)
                    if not isinstance(g, int) or g == 0:
                        pe.wait_ge(s_w[3], 48)
                else:
                    pe.wait_ge(s_hid, g * UD + i)
                for bank, w in ((4, w1), (5, w3)):
                    mm = project(ps[:, bank, :], lambda k: w[:, k, P * i:P * i + P], lambda k: hdT[:, k, :])
                mm.then_inc(s_up_ps, 1)

            def down(g, i):
                pe.wait_ge(s_hid, g * UD + i + 1)
                for j in range(T):
                    mm = pe.matmul(ps[:, 6 + j // 2, D * (j % 2):D * (j % 2) + D], hidT[:, i % 4, P * j:P * j + P],
                                   w2[:, i, :], start=(i == 0 and j % 2 == 0), stop=(i == UD - 1),
                                   skip_group_check=True)
                mm.then_inc(s_down, 1)

            def route(g):
                for j in range(T):
                    mm = project(ps[:, 4, E * j:E * j + E], lambda k: nT[:, k, P * j:P * j + P],
                                 lambda k: router[:, k, :])
                mm.then_inc(s_lg_ps, 1)

            def half(ga, gb):
                A, Bh = ga is not None, gb is not None
                if A:
                    turn_x(ga)
                if Bh:
                    score(1, gb, 0)
                if A:
                    conv(ga)
                if Bh:
                    for j in range(2):
                        turn_p(1, gb, j, 0)
                        score(1, gb, j + 1)
                        turn_p(1, gb, j, 1)
                        weigh(1, gb, j, 0)
                        weigh(1, gb, j, 1)
                if A:
                    turn_n(0, ga)
                if Bh:
                    turn_p(1, gb, 2, 0)
                    score(1, gb, 3)
                    turn_p(1, gb, 2, 1)
                    weigh(1, gb, 2, 0)
                    weigh(1, gb, 2, 1)
                    turn_p(1, gb, 3, 0)
                    turn_p(1, gb, 3, 1)
                    weigh(1, gb, 3, 0)
                    weigh(1, gb, 3, 1)
                if A:
                    queries(0, ga)
                if Bh:
                    turn_o(1, gb)
                if A:
                    keys(0, ga)
                if Bh:
                    project_o(1, gb)
                if A:
                    values(0, ga)
                if Bh:
                    pe.wait_ge(s_hd, gb + 1)
                    if A:
                        pe.wait_ge(s_k, ga * 4 + 2)
                    turn(hd, 4, s_hdT_ps)
                if A:
                    score(0, ga, 0)
                if Bh:
                    if A:
                        pe.wait_ge(s_v0, ga * 4 + 4)
                    ups(gb, 0)
                for j in range(T):
                    if A:
                        turn_p(0, ga, j, 0)
                        if j + 1 < T:
                            score(0, ga, j + 1)
                        turn_p(0, ga, j, 1)
                        weigh(0, ga, j, 0)
                    if Bh:
                        ups(gb, j + 1)
                    if A:
                        weigh(0, ga, j, 1)
                    if Bh:
                        down(gb, j)
                if A:
                    turn_o(0, ga)
                if Bh:
                    ups(gb, 5)
                    down(gb, 4)
                if A:
                    project_o(0, ga)
                if Bh:
                    ups(gb, 6)
                    down(gb, 5)
                if A:
                    turn_n(1, ga)
                if Bh:
                    ups(gb, 7)
                    down(gb, 6)
                    down(gb, 7)
                if A:
                    queries(1, ga)
                    keys(1, ga)
                    values(1, ga)
                    pe.wait_ge(s_k, ga * 4 + 3)
                    route(ga)

            pipeline(pe, half)
            pe.wait_ge(s_rt, PRIME + G * 2)
            pe.transpose(ps[:, 0, 0:P], ident[:], ident[:]).then_inc(s_end_pe, 1)

            def mproject(dst, pairs):
                last = len(pairs) - 1
                for i, ((lh, ll), (rh, rl)) in enumerate(pairs):
                    pe.matmul(dst, lh, rh, start=(i == 0), stop=False)
                    pe.matmul(dst, lh, rl, start=False, stop=False)
                    mm = pe.matmul(dst, ll, rh, start=False, stop=(i == last))
                return mm

            def mups(g, i):
                e = i // 2
                if i == 0:
                    pe.wait_ge(s_mh, g + 1)
                    pe.wait_ge(s_ml, g + 1)
                if i % 2 == 0:
                    pe.wait_ge(s_wl, e + 1)
                if i >= 2:
                    pe.wait_ge(s_mhid, PRIME + g * UE + i - 1)
                else:
                    pe.wait_ge(s_mhid, PRIME + g * UE)
                at = P * (i % 2)
                for which in range(2):
                    mm = mproject(ps[:, 2 * (i % 2) + which, :],
                                  [((wh[:, e, which, k, at:at + P], wl[:, e, which, k, at:at + P]), (mh[:, k, :], ml[:, k, :]))
                                   for k in range(C)])
                mm.then_inc(s_mup_ps, 1)

            def mdown(g, e):
                pe.wait_ge(s_mhh, g * UE + 2 * e + 2)
                pe.wait_ge(s_mhl, g * UE + 2 * e + 2)
                if e >= 2:
                    pe.wait_ge(s_moe, PRIME + g * E + e - 1)
                else:
                    pe.wait_ge(s_moe, PRIME + g * E)
                for j in range(T):
                    slot = [(2 * e + k) % 4 for k in range(C)]
                    cols = slice(P * j, P * j + P)
                    mm = mproject(ps[:, 4 + 2 * (e % 2) + j // 2, D * (j % 2):D * (j % 2) + D],
                                  [((hh[:, slot[k], cols], hl[:, slot[k], cols]), (wh[:, e, 2, k, :], wl[:, e, 2, k, :]))
                                   for k in range(C)])
                mm.then_inc(s_mdown, 1)

            pe.sem_inc(s_mdown, PRIME)
            with pe.Fori(0, G) as g:
                for i in range(3):
                    mups(g, i)
                for e in range(E):
                    if 2 * e + 3 < UE:
                        mups(g, 2 * e + 3)
                    mdown(g, e)
                    if 2 * e + 4 < UE:
                        mups(g, 2 * e + 4)

        @block.vector
        def _(dve):
            dve.memset(v[0][0:SLOT], 0.0).then_inc(s_setup, 1)
            dve.memset(v[0][SLOT:P], 0.0).then_inc(s_setup, 1)
            dve.memset(v[1][0:SLOT], 0.0).then_inc(s_setup, 1)
            dve.memset(v[1][SLOT:P], 0.0).then_inc(s_setup, 1)
            dve.wait_ge(s_setup, 4)
            for a in range(2):
                for s in range(2):
                    ins = dve.memset(v[a][SLOT * s:SLOT * s + SLOT, :, :, s, HD:VW], 1.0)
            ins.then_inc(s_setup, 1)
            dve.wait_ge(s_w[0], 80)
            dve.tensor_scalar(qscale[:], colv[:, MEVEN:MEVEN + 2], QSCALE, None, ALU.mult).then_inc(s_const, 1)
            dve.tensor_copy(identr[:], ident[:]).then_inc(s_setup, 1)
            dve.tensor_copy(maskr[:], mask[:].unsqueeze(1).broadcast_to([P, C * R // 2, SLOT])).then_inc(s_setup, 1)
            dve.wait_ge(s_const, 3)
            for c in range(C):
                ins = dve.tensor_scalar(qbias[:, c, :], qscale[:], colv[:, BQ + c:BQ + c + 1], None, ALU.mult)
            ins.then_inc(s_setup, 1)
            dve.wait_ge(s_w[1], 16)
            for c in range(XC):
                at = P * (c % 2)
                fold = dve.scalar_tensor_tensor(out=convw[:, c, at:at + P], in0=ident[:], scalar=0.5,
                                                in1=convw[:, c, at:at + P], op0=ALU.mult, op1=ALU.add)
            fold.then_inc(s_fold, 1)
            dve.sem_inc(s_rt, PRIME)

            count = {"a": 0, "b": 0}

            def link(part, g, ins):
                count[part] += 1
                s, links = (s_order_a, LINKS_A) if part == "a" else (s_order_b, LINKS_B)
                ins.then_inc(s, 1)
                dve.wait_ge(s, g * links + count[part])

            def statistics(g, h):
                for j in range(T):
                    ins = dve.bn_stats(bst[:, j, :], h[:, j, :])
                link("a", g, ins)
                dve.memset(fence[:], 0.0)
                for j in range(T):
                    ins = dve.bn_aggr(mv[:, j, :], bst[:, j, :])
                ins.then_inc(s_var, 1)

            def normalise(g, k, h, dst):
                dve.wait_ge(s_rstd, g * 3 + k + 1)
                for j in range(T):
                    ins = dve.tensor_scalar(dst[:, j, :], h[:, j, :], mv[:, j, 0:1], rstd[:, j:j + 1],
                                            ALU.subtract, ALU.mult)
                    if k:
                        ins.then_inc(s_n, 1)
                return ins

            def before(a, g, j):
                k = 4 * a + j
                dve.wait_ge(s_s_ps, g * 8 + k + 1)
                sp = ps[:, 0:2, :].rearrange("p s (r k) -> p s r k", k=SLOT)
                link("ab"[a], g, dve.tensor_reduce(mx[:], ps[:, 0:2, :].rearrange("p s (r k) -> p (s r) k", k=SLOT),
                                                   AX, ALU.max))
                past(dve, s_p, g * 8 + k)
                dve.tensor_tensor(scores[:, :, :, :].rearrange("p r s k -> p s r k"), sp,
                                  mx[:].rearrange("p (s r) -> p s r", s=2).unsqueeze(3).broadcast_to([P, 2, C * R, SLOT]),
                                  ALU.subtract).then_inc(s_s_sub, 1)

            def after(a, g, j):
                k = 4 * a + j
                dve.wait_ge(s_pv, g * 16 + 2 * k + 2)
                ov = ps[:, 3, 0:H * VW].rearrange("p (h d) -> p h d", d=VW)
                link("ab"[a], g, dve.reciprocal(rinv[:], ov[:, :, HD]))
                ov = ov.rearrange("p (r s) d -> p r s d", s=2)
                dve.tensor_tensor(o[:, j, :, :].rearrange("p s (r d) -> p r s d", d=HD), ov[:, :, :, 0:HD],
                                  rinv[:].rearrange("p (r s) -> p r s", s=2).unsqueeze(3).broadcast_to([P, C * R, 2, HD]),
                                  ALU.mult).then_inc(s_o, 1)

            def evac_k(a, g):
                for c in range(C):
                    dve.wait_ge(s_k_ps, g * 4 + 2 * a + c + 1)
                    if a == 0:
                        dve.tensor_scalar(kT[a][:, :, c, :], ps[:, 4 + c, :].rearrange("p (j k) -> p j k", k=P), colv[:, BK + c:BK + c + 1], None, ALU.add)\
                           .then_inc(s_k, 1)
                    else:
                        dve.tensor_copy(kT[a][:, :, c, :], ps[:, 4 + c, :].rearrange("p (j k) -> p j k", k=P)).then_inc(s_k, 1)

            def hidden(g, i):
                dve.wait_ge(s_gate, g * UD + i + 1)
                link("b", g, dve.scalar_tensor_tensor(out=up[:], in0=gate[:, i % 2, :], scalar=1.0, in1=ps[:, 4, :],
                                                      op0=ALU.add, op1=ALU.mult))
                if i >= 4:
                    dve.wait_ge(s_down, g * UD + i - 3)
                dve.scalar_tensor_tensor(out=hidT[:, i % 4, :], in0=up[:], scalar=0.5, in1=ps[:, 5, :],
                                         op0=ALU.mult, op1=ALU.mult).then_inc(s_hid, 1)

            def scaled(g, k, bank, vec):
                dve.wait_ge(s_rms, g * 2 + k + 1)
                if k:
                    dve.wait_ge(s_y1, g + 1)
                elif isinstance(g, int):
                    dve.wait_ge(s_y, g)
                for j in range(T):
                    ins = dve.scalar_tensor_tensor(out=rt[:, j, :], in0=ps[:, bank + j // 2, D * (j % 2):D * (j % 2) + D],
                                                   scalar=rms[:, k, j:j + 1], in1=rowv[:, vec, :],
                                                   op0=ALU.mult, op1=ALU.mult)
                ins.then_inc(s_rt, 1)

            def conv_rows(g):
                for j in range(T):
                    dve.wait_ge(s_conv, g * T + j + 1)
                    ins = dve.tensor_tensor(h0[:, j, :], ps[:, 4 + j, 0:D], rowv[:, CONV_B, :], ALU.add)
                link("a", g, ins)
                statistics(g, h0)

            def affine(g):
                link("a", g, normalise(g, 0, h0, h0))
                link("a", g, dve.tensor_tensor(h0[:], h0[:], rowv[:, GAMMA:GAMMA + 1, :].broadcast_to([P, T, D]), ALU.mult))
                link("a", g, dve.tensor_tensor(h0[:], h0[:], rowv[:, BETA:BETA + 1, :].broadcast_to([P, T, D]), ALU.add))
                statistics(g, h0)

            def evac_v(g):
                for b in range(2):
                    dve.wait_ge(s_v_ps, g * 4 + b + 1)
                    for s in range(2):
                        rows = slice(SLOT * s, SLOT * s + SLOT)
                        bias = rowv[rows, BV, :].rearrange("p (h d) -> p h d", d=HD).unsqueeze(1)\
                            .broadcast_to([SLOT, 2, H, HD])
                        dve.tensor_tensor(v[0][rows, 2 * b:2 * b + 2, :, s, 0:HD],
                                          ps[rows, 6 + b, :].rearrange("p (j h d) -> p j h d", j=2, d=HD), bias,
                                          ALU.add).then_inc(s_v0, 1)

            def residual(g):
                dve.wait_ge(s_hbo, g + 1)
                past(dve, s_y0, g)
                for j in range(T):
                    dve.wait_ge(s_wo, g * 4 + j // 2 + 1)
                    ins = dve.tensor_tensor(h[:, j, :], ps[:, 2 + j // 2, D * (j % 2):D * (j % 2) + D], h0[:, j, :],
                                            ALU.add)
                link("a", g, ins)
                statistics(g, h)

            def route_max(g):
                dve.wait_ge(s_lg_ps, g + 1)
                lp = ps[:, 4, 0:T * E].rearrange("p (j e) -> p j e", e=E)
                link("a", g, dve.tensor_reduce(rs[:], lp, AX, ALU.max))
                dve.tensor_tensor(lg[:], lp, rs[:].unsqueeze(2).broadcast_to([P, T, E]), ALU.subtract)\
                   .then_inc(s_lgs, 1)

            def route_top(g):
                dve.wait_ge(s_lge, g + 1)
                link("b", g, dve.tensor_reduce(rs[:], lg[:], AX, ALU.add))
                link("b", g, dve.reciprocal(rs[:], rs[:]))
                link("b", g, dve.tensor_tensor(pr[:], lg[:], rs[:].unsqueeze(2).broadcast_to([P, T, E]), ALU.mult))
                other = pr[:].unsqueeze(2).broadcast_to([P, T, E, E])
                own = pr[:].unsqueeze(3).broadcast_to([P, T, E, E])
                dve.tensor_tensor(gt[:].rearrange("p (j e) f -> p j e f", e=E), other, own, ALU.is_gt)
                link("b", g, dve.tensor_tensor(eq[:].rearrange("p (j e) f -> p j e f", e=E), other, own, ALU.is_equal))
                ev = eq[:].rearrange("p (j e) f -> p j (e f)", e=E)
                link("b", g, dve.tensor_tensor(ev, ev, lower[:].unsqueeze(1).broadcast_to([P, T, E * E]), ALU.mult))
                link("b", g, dve.tensor_tensor(gt[:], gt[:], eq[:], ALU.add))
                link("b", g, dve.tensor_reduce(rank[:].rearrange("p j e -> p (j e)"), gt[:], AX, ALU.add))
                dve.wait_ge(s_cst, PRIME + g * 16)
                dve.scalar_tensor_tensor(out=cw[:], in0=rank[:], scalar=1.5, in1=pr[:],
                                         op0=ALU.is_lt, op1=ALU.mult).then_inc(s_cw, 1)

            def half(ga, gb):
                count["a"] = count["b"] = 0
                A, Bh = ga is not None, gb is not None
                if A:
                    for c in range(1, XC, 2):
                        dve.wait_ge(s_xt_ps, ga * XC + c + 1)
                        dve.tensor_copy(xT[:, c, :], ps[:, 4 + c, :]).then_inc(s_xt_v, 1)
                if Bh:
                    before(1, gb, 0)
                if A:
                    conv_rows(ga)
                if Bh:
                    before(1, gb, 1)
                if A:
                    affine(ga)
                if Bh:
                    after(1, gb, 0)
                    before(1, gb, 2)
                if A:
                    normalise(ga, 1, h0, n[0])
                if Bh:
                    after(1, gb, 1)
                    before(1, gb, 3)
                    after(1, gb, 2)
                    route_top(gb)
                    after(1, gb, 3)
                if A:
                    evac_k(0, ga)
                if Bh:
                    scaled(gb, 0, 2, W_ATT)
                    dve.wait_ge(s_rt, PRIME + gb * 2 + 1)
                    dve.tensor_tensor(hd[:], rt[:], n[1][:], ALU.add).then_inc(s_hd, 1)
                if A:
                    evac_v(ga)
                    before(0, ga, 0)
                if Bh:
                    hidden(gb, 0)
                for j in range(T):
                    if A and j + 1 < T:
                        before(0, ga, j + 1)
                    if Bh:
                        hidden(gb, j + 1)
                    if A:
                        after(0, ga, j)
                if Bh:
                    hidden(gb, 5)
                if A:
                    residual(ga)
                if Bh:
                    hidden(gb, 6)
                if A:
                    normalise(ga, 2, h, n[1])
                if Bh:
                    hidden(gb, 7)
                    scaled(gb, 1, 6, W_FF)
                if A:
                    evac_k(1, ga)
                    route_max(ga)
                assert not A or count["a"] == LINKS_A, count
                assert not Bh or count["b"] == LINKS_B, count

            pipeline(dve, half)
            dve.wait_ge(s_y, G)
            dve.memset(fence[:], 0.0).then_inc(s_end_dve, 1)

            dve.wait_ge(s_end_pe, 1)
            dve.wait_ge(s_end_act, 1)
            dve.wait_ge(s_end_pool, 1)
            for e in range(E):
                dve.wait_ge(s_wh, e + 1)
                dve.tensor_tensor(wl[:, e, :, :, :], raw[:, e % 2, :, :, :], wh[:, e, :, :, :].bitcast(F32), ALU.subtract)\
                   .then_inc(s_wl, 1)
            dve.sem_inc(s_moe, PRIME)
            dve.sem_inc(s_mhid, PRIME)
            with dve.Fori(0, G) as g:
                dve.wait_ge(s_mh, g + 1)
                dve.tensor_tensor(ml[:], m_in[:], mh[:].bitcast(F32), ALU.subtract).then_inc(s_ml, 1)

                def mhidden(i):
                    dve.wait_ge(s_mgate, g * UE + i + 1)
                    dve.wait_ge(s_mhid, PRIME + g * UE + i)
                    dve.scalar_tensor_tensor(out=mup[:], in0=mgate[:, i % 2, :], scalar=1.0, in1=ps[:, 2 * (i % 2), :],
                                             op0=ALU.add, op1=ALU.mult).then_inc(s_mu, 1)
                    dve.wait_ge(s_mu, g * UE + i + 1)
                    if i >= 2:
                        dve.wait_ge(s_mhl, g * UE + i - 1)
                    dve.scalar_tensor_tensor(out=mhid[:, i % 2, :], in0=mup[:], scalar=0.5, in1=ps[:, 2 * (i % 2) + 1, :],
                                             op0=ALU.mult, op1=ALU.mult).then_inc(s_mhid, 1)

                def collect(e):
                    dve.wait_ge(s_mdown, PRIME + g * E + e + 1)
                    dve.wait_ge(s_moe, PRIME + g * E + e)
                    for j in range(T):
                        src = ps[:, 4 + 2 * (e % 2) + j // 2, D * (j % 2):D * (j % 2) + D]
                        if e == 0:
                            ins = dve.tensor_scalar(moe[:, j, :], src, mcw[:, j, e:e + 1], None, ALU.mult)
                        else:
                            ins = dve.scalar_tensor_tensor(out=moe[:, j, :], in0=src, scalar=mcw[:, j, e:e + 1],
                                                           in1=moe[:, j, :], op0=ALU.mult, op1=ALU.add)
                    ins.then_inc(s_moe, 1)

                for i in range(3):
                    mhidden(i)
                dve.wait_ge(s_my_in, g * 32 + 32)
                for e in range(E):
                    if 2 * e + 3 < UE:
                        mhidden(2 * e + 3)
                    if 2 * e + 4 < UE:
                        mhidden(2 * e + 4)
                    collect(e)
                dve.wait_ge(s_mrms, g + 1)
                for j in range(T):
                    ins = dve.scalar_tensor_tensor(out=moe2[:, j, :], in0=moe[:, j, :], scalar=mrms[:, j:j + 1],
                                                   in1=rowv[:, W_MOE, :], op0=ALU.mult, op1=ALU.mult)
                ins.then_inc(s_mt, 1)
                dve.wait_ge(s_mt, g + 1)
                dve.tensor_tensor(my[:], my[:], moe2[:], ALU.add).then_inc(s_my, 1)


def kernel(x, L0_tok_conv_w, L0_tok_conv_b, L0_tok_ln_gamma, L0_tok_ln_beta, L0_attn_Wq, L0_attn_bq, L0_attn_Wk,
           L0_attn_bk, L0_attn_Wv, L0_attn_bv, L0_attn_Wo, L0_attn_bo, L0_ffn_wq, L0_ffn_wk, L0_ffn_wv, L0_ffn_wo,
           L0_ffn_w1, L0_ffn_w2, L0_ffn_w3, L0_ffn_attn_norm_w, L0_ffn_ff_norm_w, L0_ffn_moe_norm_w, L0_ffn_router_w,
           L0_ffn_ew1, L0_ffn_ew2, L0_ffn_ew3):
    import numpy as np
    import concourse.bacc as bacc
    from concourse.bass_utils import run_bass_kernel_spmd

    def contraction_first(w):
        w = np.asarray(w)
        w = w.reshape(w.shape[:-2] + (w.shape[-2] // P, P, w.shape[-1]))
        return np.ascontiguousarray(np.moveaxis(w, -2, 0))

    def by_parity(w):
        return np.asarray(w).reshape(C * R, 2, HD, D).transpose(1, 0, 2, 3).reshape(D, D)

    def per_feature(b):
        return np.asarray(b).reshape(C, P).T

    rows = np.stack([np.asarray(b) for b in (L0_tok_conv_b, L0_tok_ln_gamma, L0_tok_ln_beta, L0_attn_bv, L0_attn_bo,
                                             L0_ffn_attn_norm_w, L0_ffn_ff_norm_w, L0_ffn_moe_norm_w)])
    even = (np.arange(P) % 32 < HD).astype(np.float32)[:, None]
    row = np.arange(P)[:, None] % SLOT
    pair = (np.arange(P)[:, None] // 32 == np.arange(R)[None, :]).astype(np.float32)
    arrays = {
        "x": np.asarray(x).reshape(G, T, 2, L, D),
        "rows": np.ascontiguousarray(np.broadcast_to(rows, (P,) + rows.shape)),
        "cols": np.concatenate([per_feature(L0_attn_bq), per_feature(L0_attn_bk), even, 1 - even, pair], axis=1),
        "ident": np.eye(P, dtype=np.float32),
        "mask": np.where(np.arange(SLOT)[None, :] <= row, 0.0, NEG).astype(np.float32),
        "lower": np.ascontiguousarray(np.broadcast_to(np.tril(np.ones((E, E), np.float32), -1).reshape(1, -1), (P, E * E))),
        "conv_w": contraction_first(np.asarray(L0_tok_conv_w).transpose(2, 1, 0).reshape(2 * D, D)),
        "attn_w": contraction_first(np.stack([np.asarray(w).T for w in (L0_attn_Wq, L0_attn_Wk, L0_attn_Wv)]
                                             + [by_parity(np.asarray(L0_attn_Wo).T)]
                                             + [np.asarray(w) for w in (L0_ffn_wq, L0_ffn_wk, L0_ffn_wv)]
                                             + [by_parity(L0_ffn_wo)])),
        "w1": contraction_first(L0_ffn_w1),
        "w3": contraction_first(L0_ffn_w3),
        "w2": contraction_first(L0_ffn_w2),
        "router": contraction_first(L0_ffn_router_w),
        "ew1": contraction_first(L0_ffn_ew1),
        "ew3": contraction_first(L0_ffn_ew3),
        "ew2": contraction_first(L0_ffn_ew2),
    }
    nc = bacc.Bacc("TRN2", target_bir_lowering=False, num_devices=1)
    arrays = {f"in_{k}": np.ascontiguousarray(a) for k, a in arrays.items()}
    aps = [nc.dram_tensor(k, a.shape, F32, kind="ExternalInput").ap() for k, a in arrays.items()]
    out = nc.dram_tensor("out", (G, T, 2, TOK, D), F32, kind="ExternalOutput").ap()
    program(nc, *aps, out)
    r = run_bass_kernel_spmd(nc, [arrays], core_ids=[0])
    return r.results[0]["out"].reshape(B, TOK, D)
```

```python
from contextlib import ExitStack

import concourse.bass as bass
from concourse import mybir

F32 = mybir.dt.float32
F32R = mybir.dt.float32r
U32 = mybir.dt.uint32
ACT = mybir.ActivationFunctionType
ALU = mybir.AluOpType
AX = mybir.AxisListType.X

P = 128
B, L, D = 64, 125, 256
TOK = (L + 1) // 2
SLOT = 64
T = 4
G = B // (2 * T)
C = D // P
GT = T * P
H, HD = 16, 16
R = 4
VW = HD + 1
FF, E = 1024, 8
UD = FF // P
CAP = B * SLOT + P
ROWS = P + E * CAP
ID, FIRST, SHARE = D, D + 1, D + 2
SENT = D + 4
NT = 2 * ((2 * B * SLOT + E * (P - 1)) // P // 2 + 1)
AHEAD, BEHIND = 8, 8
XC = 2 * D // P
EPS = 1e-5
NEG = -1e30
QSCALE = HD ** -0.5
LINKS_A, LINKS_B = 17, 27
PRIME = 1

CONV_B, GAMMA, BETA, BV, BO, W_ATT, W_FF, W_MOE = range(8)
BQ, BK, MEVEN, MODD, PAIR = 0, 2, 4, 5, 6


def program(nc, x, rows, cols, ident_in, mask_in, lower_in, before_in, marks_in, own_in, conv_w, attn_w, w1_in, w3_in, w2_in,
            router_in, ew13_in, ew2_in, out):
    ctx = ExitStack()
    with ctx:
        def dram(name, shape):
            return nc.dram_tensor(name, shape, F32, kind="Internal").ap()

        def sem(name):
            return ctx.enter_context(nc.semaphore(name))

        y_mid = dram("y_mid", (G, T, P, D))
        sent = dram("sent", (ROWS, SENT))
        back = dram("back", (2 * B * SLOT, D))

        def sb(name, shape, dt=F32):
            return ctx.enter_context(nc.sbuf_tensor(name, shape, dt))

        rowv = sb("rowv", [P, 8, D])
        nhalf = sb("nhalf", [P, T])
        epsv = sb("epsv", [P, T])
        ident = sb("ident", [P, P])
        own = sb("own", [P, T + 1])
        filled = sb("filled", [P, E])
        filledi = sb("filledi", [P, E], U32)
        tilesf = sb("tilesf", [P, 2, NT])
        tiles = sb("tiles", [P, 2, NT], U32)

        first = ExitStack()

        def s1(name, shape, dt=F32):
            return first.enter_context(nc.sbuf_tensor(name, shape, dt))

        def beneath(name, shape):
            with nc.sbuf_tensor(name, shape, F32) as a:
                return a

        x_in = s1("x_in", [P, T, 2 * D])
        convw = s1("convw", [P, XC, D])
        h0 = s1("h0", [P, T, D])
        nT = s1("nT", [P, C, GT])
        n, qE, kT, v = [], [], [], []
        for a in range(2):
            nx = s1(f"n{a}", [P, T, SENT if a else D])
            n.append(nx[:, :, 0:D])
            qE.append(s1(f"qE{a}", [P, C, 2 * T, 2, SLOT]))
            kT.append(s1(f"kT{a}", [P, T, C, P]))
            v.append(s1(f"v{a}", [P, T, H, 2, VW]))
        attnw = s1("attnw", [P, 8, C, D])
        router = s1("router", [P, C, E])
        kM = s1("kM", [P, 2, C, 2, R, SLOT])
        scores = s1("scores", [P, C * R, 2, SLOT])
        probs = s1("probs", [P, C * R, 2, SLOT])
        pT = s1("pT", [P, C, R * P])
        o = s1("o", [P, T, 2, P])
        oT = s1("oT", [P, 2, GT])

        w13 = s1("w13", [P, 2, C, FF], F32R)
        w13_whole = beneath("w13_whole", [P, 2, C, FF])
        w13_low = s1("w13_low", [P, 2, C, FF], F32R)
        w2 = s1("w2", [P, UD, D])
        colv = s1("colv", [P, 6 + R])
        qscale = s1("qscale", [P, 2])
        qbias = s1("qbias", [P, C, 2])
        identr = s1("identr", [P, P], F32R)
        maskr = s1("maskr", [P, C * R // 2, SLOT], F32R)
        mask = s1("mask", [P, SLOT])
        lower = s1("lower", [P, E * E])
        h = s1("h", [P, T, D])
        rt = s1("rt", [P, T, D])
        hd = s1("hd", [P, T, D])
        junk = beneath("junk", [P, T, D])
        hdT = s1("hdT", [P, C, GT], F32R)
        hdT_low = s1("hdT_low", [P, C, GT], F32R)
        gate = s1("gate", [P, 2, GT])
        xT = hidT = s1("xT", [P, XC, GT])
        y = s1("y", [P, T, D])
        bst = s1("bst", [P, T, 6])
        mv = s1("mv", [P, T, 2])
        vare = s1("vare", [P, T])
        rstd = s1("rstd", [P, T])
        pfence = s1("pfence", [P, 1])
        fence = s1("fence", [P, 1])
        ss = s1("ss", [P, 2, T])
        msq = s1("msq", [P, 2, T])
        rms = s1("rms", [P, 2, T])
        mx = s1("mx", [P, 2, H])
        rinv = s1("rinv", [P, H])
        lg = s1("lg", [P, T, E])
        pr = s1("pr", [P, T, E])
        rs = s1("rs", [P, T])
        gt = s1("gt", [P, T * E, E])
        eq = s1("eq", [P, T * E, E])
        rank = s1("rank", [P, T, E])
        chosen = s1("chosen", [P, T + 1, E])
        place = s1("place", [P, T, E])
        pick = s1("pick", [P, 5, T, E])
        slotf = s1("slotf", [P, 2, T])
        slot_now = s1("slot_now", [P, 2, T], U32)
        before_t = s1("before_t", [P, 2, P])
        marks = s1("marks", [P, 2 * E + 32 + NT])
        sent_n = s1("sent_n", [P, E])
        n_tiles = s1("n_tiles", [P, E])
        t_first = s1("t_first", [P, E])
        t_end = s1("t_end", [P, E])
        t_row = s1("t_row", [P, E])
        first.close()

        def s2(name, shape, dt=F32):
            return sb(name, shape, dt)

        wu_whole = beneath("wu_whole", [P, E, C, 2 * D])
        wu_low = s2("wu_low", [P, E, C, 2 * D], F32R)
        m = s2("m", [P, 4, SENT])
        zero = s2("zero", [P, SENT])
        wd = s2("wd", [P, E, C, D])
        wu = s2("wu", [P, E, C, 2 * D], F32R)
        mT = s2("mT", [P, 2, C, P], F32R)
        mT_low = s2("mT_low", [P, 2, C, P], F32R)
        mgate = s2("mgate", [P, 2, D])
        mup = s2("mup", [P, 2, D])
        mhid = s2("mhid", [P, 2, D])
        mhidT = s2("mhidT", [P, 2, C, P])
        z = s2("z", [P, 4, D])
        zg = s2("zg", [P, 2, T, 2, D])
        meta = s2("meta", [P, NT, SENT - D])
        parts = s2("parts", [P, 2, 2])
        portion = s2("portion", [P, 2])
        target = s2("target", [P, 4], U32)
        zfence = s2("zfence", [P, 1])
        moe = s2("moe", [P, 2, T, D])
        moe2 = s2("moe2", [P, 2, T, D])
        my = s2("my", [P, G * T, D])
        mjunk = s2("mjunk", [P, 2, T, D])
        mss = s2("mss", [P, 2, T])
        mms = s2("mms", [P, 2, T])
        mrms = s2("mrms", [P, 2, T])

        ps = ctx.enter_context(nc.psum_tensor("ps", [P, 8, 512], F32))

        s_w = [sem(f"s_w{i}") for i in range(4)]
        names = ("x pad const setup fold xt_ps xt_a xt_v conv order_a order_b var vare rstd n hbo nT_ps nT_a "
                 "q_ps k_ps q k km v_ps v0 v1 s_ps s_sub p pT_ps pT_a pv o oT_ps oT_a wo ss msq rms rt "
                 "hd hdT_ps hdT_a hdT_low up_ps gate hid down y0 y1 y yst lg_ps lgs lge chosen place placed slot pfence sent "
                 "ylast order_t tiles zero padded wu wd split high low yin "
                 "m_ps mT mT_low mup_ps mgate mu mhid mhT_ps mhT mdown meta parts portion target z zfence moe "
                 "mss mms mrms mt my out").split()
        sems = {name: sem("s_" + name) for name in names}
        (s_x, s_pad, s_const, s_setup, s_fold, s_xt_ps, s_xt_a, s_xt_v, s_conv, s_order_a, s_order_b, s_var, s_vare,
         s_rstd, s_n, s_hbo, s_nT_ps, s_nT_a, s_q_ps, s_k_ps, s_q, s_k, s_km, s_v_ps, s_v0, s_v1, s_s_ps,
         s_s_sub, s_p, s_pT_ps, s_pT_a, s_pv, s_o, s_oT_ps, s_oT_a, s_wo, s_ss, s_msq, s_rms, s_rt,
         s_hd, s_hdT_ps, s_hdT_a, s_hdT_low, s_up_ps, s_gate, s_hid, s_down, s_y0, s_y1, s_y, s_yst,
         s_lg_ps, s_lgs, s_lge, s_chosen, s_place, s_placed, s_slot, s_pfence, s_sent, s_ylast,
         s_order_t, s_tiles, s_zero, s_padded, s_wu, s_wd, s_split, s_high, s_low, s_yin, s_m_ps, s_mT, s_mT_low, s_mup_ps,
         s_mgate, s_mu, s_mhid, s_mhT_ps, s_mhT, s_mdown, s_meta, s_parts, s_portion, s_target, s_z, s_zfence, s_moe, s_mss, s_mms,
         s_mrms, s_mt, s_my, s_out) = (sems[name] for name in names)

        s_m = [sem(f"s_m{i}") for i in range(4)]
        s_back = [sem(f"s_back{i}") for i in range(4)]
        s_got = [sem(f"s_got{i}") for i in range(2)]

        block = ctx.enter_context(nc.Block())

        def head(c, r, e):
            return 8 * c + 2 * r + e

        def past(eng, s, value):
            if not (isinstance(value, int) and value <= 0):
                eng.wait_ge(s, value)

        def pipeline(eng, half):
            half(0, None)
            with eng.Fori(0, G - 1) as g:
                half(g + 1, g)
            half(None, G - 1)

        def tile_pipeline(eng, beat, first=None):
            for b in range(-1, AHEAD - 1):
                beat(b, b % 4)
            with eng.Fori(0, (NT + 4 - AHEAD - BEHIND) // 4) as i:
                if first:
                    first(4 * i + (AHEAD - 1))
                for r in range(4):
                    beat(4 * i + (AHEAD - 1 + r), (AHEAD - 1 + r) % 4)
            for b in range(NT + 3 - BEHIND, NT + 3):
                beat(b, b % 4)

        def quarter(t, k):
            return (t - k) * 4 + 16

        def attention_ended(eng):
            eng.wait_ge(s_wo, G * 4)
            eng.wait_ge(s_hd, G)
            eng.wait_ge(s_y0, G)
            eng.wait_ge(s_sent, G * 2 * T * 16)
            eng.wait_ge(s_tiles, 1)

        def first_phase_ended(eng):
            eng.wait_ge(s_down, G * UD)
            eng.wait_ge(s_ss, G * 2 * T)
            eng.wait_ge(s_rt, PRIME + G * 2)
            eng.wait_ge(s_y, G)
            eng.wait_ge(s_ylast, 16)

        def unit_bank(g, i):
            return 0 if isinstance(g, int) and g == G - 1 and i % 2 else 4

        def alone(a, g):
            return isinstance(g, int) and g == (G - 1 if a else 0)

        def score_bank(a, g, j):
            return 6 if alone(a, g) and j % 2 else 0

        def real(t):
            return not isinstance(t, int) or 0 <= t < NT

        @block.sync
        def _(sp):
            def load_x(g):
                for s in range(2):
                    src = x[g, :, s]
                    sp.dma_start(x_in[SLOT * s:SLOT * s + TOK - 1, :, :],
                                 src[:, 0:L - 1, :].rearrange("j (t k) i -> t j (k i)", k=2)).then_inc(s_x, 16)
                    sp.dma_start(x_in[SLOT * s + TOK - 1:SLOT * s + TOK, :, 0:D],
                                 src[:, L - 1:L, :].rearrange("j t i -> t j i")).then_inc(s_x, 16)

            def save_b(g):
                sp.wait_ge(s_y, g + 1)
                sp.dma_start(y_mid[g].rearrange("j p i -> p j i"), y[:]).then_inc(s_yst, 16)

            sp.dma_start(ident[:], ident_in).then_inc(s_w[0], 16)
            sp.dma_start(mask[:], mask_in).then_inc(s_w[0], 16)
            sp.dma_start(lower[:], lower_in).then_inc(s_w[0], 16)
            sp.dma_start(colv[:], cols).then_inc(s_w[0], 16)
            sp.dma_start(rowv[:], rows).then_inc(s_w[0], 16)
            sp.dma_start(own[:], own_in).then_inc(s_w[0], 16)
            sp.sem_inc(s_yst, PRIME)
            sp.wait_ge(s_pad, 2)
            load_x(0)
            sp.dma_start(convw[:], conv_w).then_inc(s_w[1], 16)
            sp.dma_start(attnw[:], attn_w).then_inc(s_w[2], 16)
            sp.dma_start(router[:], router_in).then_inc(s_w[2], 16)
            for i, w in enumerate((w1_in, w3_in)):
                sp.dma_start(w13_whole[:, i, :, :], w).then_inc(s_w[3], 16)
            sp.dma_start(w2[:], w2_in).then_inc(s_w[3], 16)
            sp.dma_start(before_t[:], before_in).then_inc(s_w[3], 16)
            sp.dma_start(marks[:], marks_in).then_inc(s_w[3], 16)
            sp.wait_ge(s_xt_ps, XC)
            load_x(1)
            with sp.Fori(0, G - 2) as g:
                sp.wait_ge(s_xt_ps, g * XC + 2 * XC)
                load_x(g + 2)
                save_b(g)
            save_b(G - 2)

            sp.wait_ge(s_v_ps, G * 4)
            sp.wait_ge(s_lg_ps, G)
            sp.wait_ge(s_lgs, G)
            sp.wait_ge(s_lge, G)
            sp.wait_ge(s_rstd, G * 3)
            sp.dma_start(wu_whole[:], ew13_in).then_inc(s_wu, 16)

            sp.wait_ge(s_zero, 1)
            sp.wait_ge(s_tiles, 1)
            sp.dma_start(sent[0:P, :], zero[:]).then_inc(s_padded, 16)
            for e in range(E):
                end = sp.value_load(filledi[0:1, e:e + 1], min_val=P + e * CAP, max_val=(e + 1) * CAP)
                sp.dma_start(sent[bass.ds(end, P), :], zero[:]).then_inc(s_padded, 16)
            sp.wait_ge(s_padded, 16 * (E + 1))
            sp.wait_ge(s_sent, G * 2 * T * 16)

            def row(t):
                return sp.value_load(tiles[0:1, 0, bass.ds(t, 1)], min_val=0, max_val=ROWS - P)

            attention_ended(sp)
            sp.dma_start(wd[:], ew2_in).then_inc(s_wd, 16)
            y_rows = y_mid.rearrange("g j p i -> (g j) p i")
            for t in range(4):
                sp.dma_start(m[:, t, :], sent[bass.ds(row(t), P), :]).then_inc(s_m[t], 16)

            def beat(b, four):
                r = four % 2
                if real(b + 5):
                    at = row(b + 5)
                    turned = b + 2 if isinstance(b, int) else sp.snap(b + 2)
                    sp.wait_ge(s_meta, turned)
                    sp.wait_ge(s_m_ps, turned)
                    k = (four + 1) % 4
                    sp.dma_start(m[:, k, :], sent[bass.ds(at, P), :]).then_inc(s_m[k], 16)

                if isinstance(b, int) and b == AHEAD - 2:
                    first_phase_ended(sp)
                    sp.wait_ge(s_yst, PRIME + (G - 1) * 16)
                elif not isinstance(b, int) and r:
                    i = (b - (AHEAD - 1)) // 2
                    sp.dma_start(my[:, bass.ds(i, 1), :].rearrange("p g i -> p (g i)"), y_rows[i]).then_inc(s_yin, 16)

            tile_pipeline(sp, beat)
            for i in range((NT + 4 - AHEAD - BEHIND) // 2, G * T):
                sp.dma_start(my[:, i, :], y_rows[i]).then_inc(s_yin, 16)

            pairs = back.rearrange("(g p x) i -> g p (x i)", p=P, x=2 * T)

            def load_pairs(g, r):
                sp.dma_start(zg[:, r, :, :, :].rearrange("p j k i -> p (j k i)"), pairs[g]).then_inc(s_got[r], 16)

            for s in s_back:
                sp.wait_ge(s, NT // 4 * 16)
            for r in range(2):
                load_pairs(r, r)
            with sp.Fori(0, G // 2 - 1) as i:
                for r in range(2):
                    sp.wait_ge(s_moe, 2 * i + r + 1)
                    load_pairs(2 * i + r + 2, r)
            sp.wait_ge(s_out, G * 32)

        @block.gpsimd
        def _(pool):
            pool.memset(x_in[:, 0:2, :], 0.0).then_inc(s_pad, 1)
            pool.memset(x_in[:, 2:4, :], 0.0).then_inc(s_pad, 1)
            pool.memset(nhalf[:], -0.5).then_inc(s_const, 1)
            pool.memset(epsv[:], EPS).then_inc(s_const, 1)
            pool.memset(pfence[:], 0.0).then_inc(s_pfence, 1)
            pool.wait_ge(s_const, 2)
            pool.wait_ge(s_w[0], 96)

            def power(g, k):
                pool.wait_ge(s_var, g * 3 + k + 1)
                pool.tensor_tensor(vare[:], mv[:, :, 1], epsv[:], ALU.add).then_inc(s_vare, 1)
                pool.wait_ge(s_vare, g * 3 + k + 1)
                pool.tensor_tensor(rstd[:], vare[:], nhalf[:], ALU.pow).then_inc(s_rstd, 1)

            def rms_power(g, k):
                pool.wait_ge(s_ss, g * (2 * T) + T * (k + 1))
                pool.tensor_tensor(msq[:, k, :], ss[:, k, :], epsv[:], ALU.add).then_inc(s_msq, 1)
                pool.wait_ge(s_msq, g * 2 + k + 1)
                pool.tensor_tensor(rms[:, k, :], msq[:, k, :], nhalf[:], ALU.pow).then_inc(s_rms, 1)

            def mask_keys(a, g, j):
                k = 4 * a + j
                if j == 0:
                    pool.wait_ge(s_k, g * 4 + 2 * a + 2)
                past(pool, s_s_ps, g * 8 + k - 1)
                src = kT[a][:, j, :, :].rearrange("p c (s k) -> p (c s) k", s=2).unsqueeze(2).broadcast_to([P, 2 * C, R, SLOT])
                own = colv[:, PAIR:PAIR + R].unsqueeze(1).unsqueeze(3).broadcast_to([P, 2 * C, R, SLOT])
                pool.tensor_tensor(kM[:, j % 2, :, :, :, :].rearrange("p c s r k -> p (c s) r k"), src, own, ALU.mult)\
                    .then_inc(s_km, 1)

            def send(g):
                pool.wait_ge(s_slot, g + 1)
                pool.tensor_tensor(pfence[:], pfence[:], pfence[:], ALU.add).then_inc(s_pfence, 1)
                for k in range(2):
                    for j in range(T):
                        pool.indirect_dma_start(out=sent[:, :], in_=nx[:, j, :], in_offset=None,
                                                out_offset=bass.IndirectOffsetOnAxis(ap=slot_now[:, k, j:j + 1], axis=0))\
                            .then_inc(s_sent, 16)

            def half(ga, gb):
                if gb is not None:
                    mask_keys(1, gb, 0)
                    mask_keys(1, gb, 1)
                    pool.wait_ge(s_yst, PRIME + gb * 16)
                    pool.tensor_tensor(y[:], h[:], n[1][:], ALU.add).then_inc(s_y0, 1)
                if gb is not None:
                    mask_keys(1, gb, 2)
                    mask_keys(1, gb, 3)
                if ga is not None:
                    power(ga, 0)
                    power(ga, 1)
                if gb is not None:
                    rms_power(gb, 0)
                if ga is not None:
                    mask_keys(0, ga, 0)
                    mask_keys(0, ga, 1)
                if gb is not None:
                    pool.wait_ge(s_y0, gb + 1)
                    pool.wait_ge(s_rt, PRIME + gb * 2 + 1)
                    pool.tensor_tensor(y[:], y[:], rt[:], ALU.add).then_inc(s_y1, 1)
                if ga is not None:
                    pool.wait_ge(s_n, ga * (2 * T) + T)
                    pool.tensor_tensor(h0[:], h0[:], rowv[:, BO:BO + 1, :].broadcast_to([P, T, D]), ALU.add)\
                        .then_inc(s_hbo, 1)
                    mask_keys(0, ga, 2)
                    mask_keys(0, ga, 3)
                if gb is None:
                    for i in range(2):
                        pool.wait_ge(s_split, 2 + i)
                        pool.tensor_tensor(w13_low[:, i, :, :], w13_whole[:, i, :, :], w13[:, i, :, :].bitcast(F32), ALU.subtract)\
                            .then_inc(s_split, 1)
                if gb is not None:
                    send(gb)
                if ga is None:
                    for e in range(E):
                        pool.wait_ge(s_high, e + 1)
                        pool.tensor_tensor(wu_low[:, e, :, :], wu_whole[:, e, :, :], wu[:, e, :, :].bitcast(F32),
                                           ALU.subtract).then_inc(s_low, 1)
                if ga is not None:
                    power(ga, 2)
                if gb is not None:
                    rms_power(gb, 1)
                    pool.wait_ge(s_y1, gb + 1)
                    pool.wait_ge(s_rt, PRIME + gb * 2 + 2)
                    pool.tensor_tensor(y[:], y[:], rt[:], ALU.add).then_inc(s_y, 1)

            pipeline(pool, half)
            pool.wait_ge(s_y, G)
            pool.dma_start(y_mid[G - 1].rearrange("j p i -> p j i"), y[:]).then_inc(s_ylast, 16)

            attention_ended(pool)

            def beat(b, four):
                r = four % 2
                if real(b - 3):
                    k = (four - 3) % 4
                    pool.wait_ge(s_target, b - 2)
                    if not isinstance(b, int) or b >= 4:
                        pool.wait_ge(s_zfence, b - 3)
                    pool.wait_ge(s_z, b - 2)
                    pool.tensor_tensor(zfence[:], nhalf[:, 0:1], nhalf[:, 0:1], ALU.add).then_inc(s_zfence, 1)
                    pool.indirect_dma_start(out=back[:, :], in_=z[:, k, :], in_offset=None,
                                            out_offset=bass.IndirectOffsetOnAxis(ap=target[:, k:k + 1], axis=0),
                                            bounds_check=2 * B * SLOT - 1, oob_is_err=False)\
                        .then_inc(s_back[k], 16)

            tile_pipeline(pool, beat)

            def moe_power(g, r):
                pool.wait_ge(s_mss, g * T + T)
                pool.tensor_tensor(mms[:, r, :], mss[:, r, :], epsv[:], ALU.add).then_inc(s_mms, 1)
                pool.wait_ge(s_mms, g + 1)
                pool.tensor_tensor(mrms[:, r, :], mms[:, r, :], nhalf[:], ALU.pow).then_inc(s_mrms, 1)

            with pool.Fori(0, G // 2) as i:
                for r in range(2):
                    moe_power(2 * i + r, r)

        @block.scalar
        def _(act):
            act.wait_ge(s_w[0], 96)
            act.wait_ge(s_setup, 9)

            def exps(a, g, j):
                act.wait_ge(s_s_sub, g * 8 + 4 * a + j + 1)
                act.activation(probs[:], scores[:], ACT.Exp).then_inc(s_p, 1)

            def evac(a, g, j):
                k = 4 * a + j
                for c in range(C):
                    act.wait_ge(s_pT_ps, g * 16 + 2 * k + c + 1)
                    past(act, s_pv, g * 16 + 2 * k + c - 1)
                    act.activation(pT[:, c, :], ps[:, 2, :], ACT.Copy).then_inc(s_pT_a, 1)

            def evac_n(a, g):
                for c in range(C):
                    act.wait_ge(s_nT_ps, g * 4 + 2 * a + c + 1)
                    act.activation(nT[:, c, :], ps[:, c, :], ACT.Copy).then_inc(s_nT_a, 1)

            def evac_q(a, g):
                bank = 0 if a else 6
                for c in range(C):
                    act.wait_ge(s_q_ps, g * 4 + 2 * a + c + 1)
                    src = ps[:, bank + c, :].rearrange("p (t q) -> p t q", q=SLOT)
                    for e in range(2):
                        ins = act.activation(qE[a][:, c, :, e, :], src, ACT.Identity, scale=qscale[:, e:e + 1],
                                             bias=0.0 if a else qbias[:, c, e:e + 1])
                    ins.then_inc(s_q, 1)

            def evac_v(g):
                for b in range(2):
                    act.wait_ge(s_v_ps, g * 4 + 2 + b + 1)
                    for s in range(2):
                        rows = slice(SLOT * s, SLOT * s + SLOT)
                        act.activation(v[1][rows, 2 * b:2 * b + 2, :, s, 0:HD].rearrange("p j h d -> p (j h) d"),
                                       ps[rows, 2 + b, :].rearrange("p (h d) -> p h d", d=HD), ACT.Copy)\
                            .then_inc(s_v1, 1)

            def evac_o(a, g):
                for b in range(2):
                    act.wait_ge(s_oT_ps, g * 4 + 2 * a + b + 1)
                    act.activation(oT[:, :, 2 * P * b:2 * P * (b + 1)].rearrange("p e (t q) -> p t e q", q=SLOT),
                                   ps[:, b, :].rearrange("p (t e q) -> p t e q", e=2, q=SLOT), ACT.Copy).then_inc(s_oT_a, 1)

            def gates(g, i):
                act.wait_ge(s_up_ps, g * UD + i + 1)
                if i >= 2:
                    act.wait_ge(s_hid, g * UD + i - 1)
                act.activation(gate[:, i % 2, :], ps[:, unit_bank(g, i), :], ACT.Tanh, scale=0.5).then_inc(s_gate, 1)
                if isinstance(g, int) and g == G - 1:
                    act.wait_ge(s_wu, 16)
                    act.activation(wu[:, i, :, :], wu_whole[:, i, :, :], ACT.Copy).then_inc(s_high, 1)

            def squares(g, k):
                for j in range(T):
                    if k == 0:
                        act.wait_ge(s_wo, g * 4 + 2 + j // 2 + 1)
                        src = ps[:, 2 + j // 2, D * (j % 2):D * (j % 2) + D]
                    else:
                        act.wait_ge(s_down, g * UD + UD)
                        src = ps[:, 6 + j // 2, D * (j % 2):D * (j % 2) + D]
                    act.activation(junk[:, j, :], src, ACT.Square, scale=D ** -0.5,
                                   accum_out=ss[:, k, j:j + 1]).then_inc(s_ss, 1)

            def half(ga, gb):
                A, Bh = ga is not None, gb is not None
                if A:
                    for c in range(0, XC, 2):
                        act.wait_ge(s_xt_ps, ga * XC + c + 1)
                        act.activation(xT[:, c, :], ps[:, 4 + c, :], ACT.Copy).then_inc(s_xt_a, 1)
                if Bh:
                    exps(1, gb, 0)
                    evac_v(gb)
                    for j in range(T):
                        evac(1, gb, j)
                        if j + 1 < T:
                            exps(1, gb, j + 1)
                    evac_o(1, gb)
                    squares(gb, 0)
                if A:
                    evac_n(0, ga)
                    evac_q(0, ga)
                if A and not Bh:
                    act.wait_ge(s_w[3], 80)
                    for i in range(2):
                        act.activation(w13[:, i, :, :], w13_whole[:, i, :, :], ACT.Copy).then_inc(s_split, 1)
                if Bh:
                    for c in range(C):
                        act.wait_ge(s_hdT_ps, gb * 2 + c + 1)
                        act.activation(hdT[:, c, :], ps[:, 4 + c, :], ACT.Copy).then_inc(s_hdT_a, 1)
                if A:
                    exps(0, ga, 0)
                if Bh:
                    gates(gb, 0)
                for j in range(T):
                    if A:
                        evac(0, ga, j)
                        if j + 1 < T:
                            exps(0, ga, j + 1)
                    if Bh:
                        gates(gb, j + 1)
                if A:
                    evac_o(0, ga)
                if Bh:
                    gates(gb, 5)
                    gates(gb, 6)
                if Bh:
                    gates(gb, 7)
                if A:
                    evac_n(1, ga)
                if Bh:
                    squares(gb, 1)
                if A:
                    evac_q(1, ga)
                    act.wait_ge(s_lgs, ga + 1)
                    act.activation(lg[:], lg[:], ACT.Exp).then_inc(s_lge, 1)

            pipeline(act, half)

            attention_ended(act)

            def beat(b, four):
                r = four % 2
                if real(b - 3):
                    q, k = 1 - r, (four - 3) % 4
                    act.wait_ge(s_mdown, b - 2)
                    if not isinstance(b, int) or b >= 7:
                        act.wait_ge(s_back[k], quarter(b - 7, k))
                    act.wait_ge(s_portion, b - 2)
                    act.activation(z[:, k, :], ps[:, 6 + q, 0:D], ACT.Identity, scale=portion[:, q:q + 1], bias=0.0)\
                       .then_inc(s_z, 1)
                if real(b - 2):
                    act.wait_ge(s_mhT_ps, b - 1)
                    if not isinstance(b, int) or b >= 4:
                        act.wait_ge(s_mdown, b - 3)
                    act.activation(mhidT[:, r, :, :].rearrange("p c k -> p (c k)"), ps[:, 4 + r, 0:D], ACT.Copy)\
                       .then_inc(s_mhT, 1)
                if real(b + 1):
                    act.wait_ge(s_m_ps, b + 2)
                    if not isinstance(b, int) or b >= 1:
                        act.wait_ge(s_mup_ps, b)
                    act.activation(mT[:, 1 - r, :, :].rearrange("p c k -> p (c k)"), ps[:, 2 + 1 - r, 0:D], ACT.Copy)\
                       .then_inc(s_mT, 1)
                if real(b):
                    act.wait_ge(s_mup_ps, b + 1)
                    if not isinstance(b, int) or b >= 2:
                        act.wait_ge(s_mhid, b - 1)
                    act.activation(mgate[:, r, :], ps[:, r, 0:D], ACT.Tanh, scale=0.5).then_inc(s_mgate, 1)

            tile_pipeline(act, beat)

            first_phase_ended(act)

            def mean_squares(g, r, first):
                act.wait_ge(s_moe, g + 1)
                if not first:
                    act.wait_ge(s_mrms, g - 1)
                for j in range(T):
                    act.activation(mjunk[:, r, j, :], moe[:, r, j, :], ACT.Square, scale=D ** -0.5,
                                   accum_out=mss[:, r, j:j + 1]).then_inc(s_mss, 1)

            def store(g):
                for s in range(2):
                    rows = slice(SLOT * s, SLOT * s + TOK)
                    act.wait_ge(s_my, g + 1)
                    act.dma_start(out[g, :, s].rearrange("j t i -> t j i"), my[rows, bass.ds(g * T, T), :]).then_inc(s_out, 16)

            for r in range(2):
                mean_squares(r, r, True)
            with act.Fori(0, G // 2 - 1) as i:
                for r in range(2):
                    mean_squares(2 * i + r + 2, r, False)
                    store(2 * i + r)
            for r in range(2):
                store(G - 2 + r)

        @block.tensor
        def _(pe):
            pe.wait_ge(s_w[0], 96)
            pe.wait_ge(s_setup, 9)

            def project(dst, left, right, chunks=C):
                for c in range(chunks):
                    mm = pe.matmul(dst, left(c), right(c), start=(c == 0), stop=(c == chunks - 1))
                return mm

            def turn(src, bank, done, chunks=C):
                for c in range(chunks):
                    for j in range(T):
                        mm = pe.transpose(ps[:, bank + c, P * j:P * j + P], src[:, j, P * c:P * c + P], ident[:])
                    mm.then_inc(done, 1)

            def turn_x(g):
                pe.wait_ge(s_x, g * 64 + 64)
                if not isinstance(g, int):
                    pe.wait_ge(s_k, g * 4)
                    pe.wait_ge(s_lgs, g)
                if not isinstance(g, int):
                    pe.wait_ge(s_rt, PRIME + (g - 1) * 2)
                turn(x_in, 4, s_xt_ps, XC)

            def conv(g, tiles_of):
                if isinstance(g, int):
                    pe.wait_ge(s_fold, 1)
                pe.wait_ge(s_xt_a, g * 2 + 2)
                pe.wait_ge(s_xt_v, g * 2 + 2)
                for j in tiles_of:
                    project(ps[:, 4 + j, 0:D], lambda c: xT[:, c, P * j:P * j + P], lambda c: convw[:, c, :], XC)\
                        .then_inc(s_conv, 1)

            def turn_n(a, g):
                pe.wait_ge(s_n, g * (2 * T) + T * (a + 1))
                if a:
                    pe.wait_ge(s_oT_a, g * 4 + 2)
                turn(n[a], 0, s_nT_ps)

            def queries(a, g):
                pe.wait_ge(s_nT_a, g * 4 + 2 * a + 2)
                if a == 0 and isinstance(g, int):
                    pe.wait_ge(s_w[2], 32)
                for c in range(C):
                    project(ps[:, (0 if a else 6) + c, :], lambda k: attnw[:, 4 * a, k, P * c:P * c + P],
                            lambda k: nT[:, k, :]).then_inc(s_q_ps, 1)

            def keys(a, g):
                for c in range(C):
                    project(ps[:, 4 + c, :], lambda k: attnw[:, 4 * a + 1, k, P * c:P * c + P],
                            lambda k: nT[:, k, :]).then_inc(s_k_ps, 1)

            def values(a, g):
                if a == 0:
                    pe.wait_ge(s_q, g * 4 + 2)
                for j in range(T):
                    bank = (2 if a else 6) + j // 2
                    mm = project(ps[:, bank, D * (j % 2):D * (j % 2) + D], lambda k: nT[:, k, P * j:P * j + P],
                                 lambda k: attnw[:, 4 * a + 2, k, :])
                    if j % 2:
                        mm.then_inc(s_v_ps, 1)

            def score(a, g, j):
                k = 4 * a + j
                if j == 0:
                    if a == 0:
                        past(pe, s_oT_a, g * 4)
                        past(pe, s_placed, g)
                    else:
                        pe.wait_ge(s_q, g * 4 + 4)
                elif not alone(a, g):
                    pe.wait_ge(s_s_sub, g * 8 + k)
                elif j >= 2:
                    pe.wait_ge(s_s_sub, g * 8 + k - 1)
                elif a:
                    pe.wait_ge(s_rt, PRIME + g * 2)
                else:
                    pe.wait_ge(s_v0, g * 4 + 4)
                bank = score_bank(a, g, j)
                for s in range(2):
                    for c in range(C):
                        pe.matmul(ps[:, bank + s, R * SLOT * c:R * SLOT * (c + 1)], identr[:], maskr[:], start=(c == 0),
                                  stop=False, skip_group_check=True)
                pe.wait_ge(s_km, g * 8 + k + 1)
                if j == 0 and a == 0:
                    pe.wait_ge(s_q, g * 4 + 2)
                for s in range(2):
                    for c in range(C):
                        mm = pe.matmul(ps[:, bank + s, R * SLOT * c:R * SLOT * (c + 1)], qE[a][:, c, 2 * j + s, :, :],
                                       kM[:, j % 2, c, s, :, :], start=False, stop=True, skip_group_check=True)
                mm.then_inc(s_s_ps, 1)

            def turn_p(a, g, j, c):
                k = 4 * a + j
                if c == 0:
                    pe.wait_ge(s_p, g * 8 + k + 1)
                    if j == 0 and a == 0:
                        past(pe, s_hd, g)
                    if j == 0 and a == 1:
                        pe.wait_ge(s_v1, g * 4 + 4)
                    if j > 0:
                        pe.wait_ge(s_pT_a, g * 16 + 2 * k)
                else:
                    pe.wait_ge(s_pT_a, g * 16 + 2 * k + 1)
                for r in range(R):
                    mm = pe.transpose(ps[:, 2, P * r:P * r + P], probs[:, R * c + r, :, :], ident[:])
                mm.then_inc(s_pT_ps, 1)

            def weigh(a, g, j, c):
                k = 4 * a + j
                pe.wait_ge(s_pT_a, g * 16 + 2 * k + c + 1)
                if c == 0 and j == 0:
                    pe.wait_ge(s_v1 if a else s_v0, g * 4 + 4)
                if c == 0 and j > 0:
                    pe.wait_ge(s_o, g * 8 + k)
                for r in range(R):
                    for e in range(2):
                        at = 2 * VW * (R * c + r)
                        mm = pe.matmul(ps[SLOT * e:SLOT * e + SLOT, 3, at:at + 2 * VW],
                                       pT[:, c, P * r + SLOT * e:P * r + SLOT * e + SLOT], v[a][:, j, head(c, r, e), :, :],
                                       start=True, stop=True)
                mm.then_inc(s_pv, 1)

            def turn_o(a, g):
                pe.wait_ge(s_o, g * 8 + 4 * a + 4)
                for b in range(2):
                    for t in range(4):
                        mm = pe.transpose(ps[:, b, P * t:P * t + P], o[:, 2 * b + t // 2, t % 2, :], ident[:])
                    mm.then_inc(s_oT_ps, 1)

            def project_o(a, g):
                pe.wait_ge(s_oT_a, g * 4 + 2 * a + 2)
                for j in range(T):
                    mm = project(ps[:, 2 + j // 2, D * (j % 2):D * (j % 2) + D], lambda e: oT[:, e, P * j:P * j + P],
                                 lambda e: attnw[:, 4 * a + 3, e, :])
                    if j % 2:
                        mm.then_inc(s_wo, 1)

            def ups(g, i):
                if i == 0:
                    pe.wait_ge(s_hdT_low, g * 2 + 2)
                    if not isinstance(g, int) or g == 0:
                        pe.wait_ge(s_w[3], 80)
                        pe.wait_ge(s_split, 4)
                elif unit_bank(g, 1) == 4:
                    pe.wait_ge(s_hid, g * UD + i)
                elif i >= 2:
                    pe.wait_ge(s_hid, g * UD + i - 1)
                else:
                    pe.wait_ge(s_placed, g + 1)
                for which in range(2):
                    to = ps[:, unit_bank(g, i) + which, :]
                    for k in range(C):
                        high, low = (w[:, which, k, P * i:P * i + P] for w in (w13, w13_low))
                        pe.matmul(to, high, hdT[:, k, :], start=(k == 0), stop=False)
                        pe.matmul(to, high, hdT_low[:, k, :], start=False, stop=False)
                        mm = pe.matmul(to, low, hdT[:, k, :], start=False, stop=(k == C - 1))
                mm.then_inc(s_up_ps, 1)

            def down(g, i):
                pe.wait_ge(s_hid, g * UD + i + 1)
                for j in range(T):
                    mm = pe.matmul(ps[:, 6 + j // 2, D * (j % 2):D * (j % 2) + D], hidT[:, i % 4, P * j:P * j + P],
                                   w2[:, i, :], start=(i == 0 and j % 2 == 0), stop=(i == UD - 1),
                                   skip_group_check=True)
                mm.then_inc(s_down, 1)

            def route(g):
                for j in range(T):
                    mm = project(ps[:, 4, E * j:E * j + E], lambda k: nT[:, k, P * j:P * j + P],
                                 lambda k: router[:, k, :])
                mm.then_inc(s_lg_ps, 1)

            def place_rows(g):
                pe.wait_ge(s_chosen, g + 1)
                pe.wait_ge(s_w[3], 80)
                to = ps[:, 0, 0:(T + 1) * E]
                pe.matmul(to, before_t[:, 0, :], chosen[:].rearrange("p j e -> p (j e)"), start=True, stop=False,
                          skip_group_check=True)
                for j in range(T):
                    later = T - j
                    mm = pe.matmul(ps[:, 0, (j + 1) * E:(T + 1) * E].rearrange("p (j e) -> p j e", e=E),
                                   before_t[:, 1, :], chosen[:, j:j + 1, :].broadcast_to([P, later, E]),
                                   start=False, stop=(j == T - 1), skip_group_check=True)
                mm.then_inc(s_place, 1)

            def half(ga, gb):
                A, Bh = ga is not None, gb is not None
                if A:
                    turn_x(ga)
                if Bh:
                    score(1, gb, 0)
                    values(1, gb)
                if not A:
                    score(1, gb, 1)
                if A:
                    conv(ga, (0,))
                for j in range(T):
                    if Bh:
                        turn_p(1, gb, j, 0)
                        ahead = j + 1 if A else j + 2
                        if ahead < T:
                            score(1, gb, ahead)
                        turn_p(1, gb, j, 1)
                        weigh(1, gb, j, 0)
                        weigh(1, gb, j, 1)
                    if A and j + 1 < T:
                        conv(ga, (j + 1,))
                if Bh:
                    turn_o(1, gb)
                if not A:
                    pe.wait_ge(s_oT_a, gb * 4 + 4)
                    place_rows(gb)
                if Bh:
                    project_o(1, gb)
                if A:
                    turn_n(0, ga)
                    queries(0, ga)
                if A and Bh:
                    place_rows(gb)
                if A:
                    keys(0, ga)
                    values(0, ga)
                if Bh:
                    pe.wait_ge(s_hd, gb + 1)
                    if A:
                        pe.wait_ge(s_k, ga * 4 + 2)
                    turn(hd, 4, s_hdT_ps)
                if A:
                    score(0, ga, 0)
                if not Bh:
                    score(0, ga, 1)
                if Bh:
                    if A:
                        pe.wait_ge(s_v0, ga * 4 + 4)
                    ups(gb, 0)
                for j in range(T):
                    if A:
                        turn_p(0, ga, j, 0)
                        ahead = j + 1 if Bh else j + 2
                        if ahead < T:
                            score(0, ga, ahead)
                        turn_p(0, ga, j, 1)
                        weigh(0, ga, j, 0)
                    if Bh:
                        ups(gb, j + 1)
                    if A:
                        weigh(0, ga, j, 1)
                    if Bh:
                        down(gb, j)
                if A:
                    turn_o(0, ga)
                if Bh:
                    ups(gb, 5)
                    down(gb, 4)
                if A:
                    project_o(0, ga)
                if Bh:
                    ups(gb, 6)
                    down(gb, 5)
                if Bh:
                    ups(gb, 7)
                    down(gb, 6)
                if A:
                    turn_n(1, ga)
                if Bh:
                    down(gb, 7)
                if A:
                    queries(1, ga)
                    keys(1, ga)
                    pe.wait_ge(s_k, ga * 4 + 3)
                    route(ga)

            pipeline(pe, half)

            def turn_m(t, r, k):
                pe.wait_ge(s_m[k], quarter(t, k))
                if not isinstance(t, int) or t >= 2:
                    pe.wait_ge(s_mT_low, t - 1)
                for c in range(C):
                    mm = pe.transpose(ps[:, 2 + r, P * c:P * c + P], m[:, k, P * c:P * c + P], ident[:])
                mm.then_inc(s_m_ps, 1)

            def expert(t):
                return pe.value_load(tiles[0:1, 1, bass.ds(t, 1)], min_val=0, max_val=E - 1)

            def mups(t, r, e):
                pe.wait_ge(s_mT_low, t + 1)
                if not isinstance(t, int) or t >= 2:
                    pe.wait_ge(s_mhid, t - 1)
                else:
                    pe.wait_ge(s_low, E)
                for c in range(C):
                    high, low = (w[:, bass.ds(e, 1), c, :].rearrange("p e i -> p (e i)") for w in (wu, wu_low))
                    pe.matmul(ps[:, r, :], mT[:, r, c, :], high, start=(c == 0), stop=False)
                    pe.matmul(ps[:, r, :], mT[:, r, c, :], low, start=False, stop=False)
                    mm = pe.matmul(ps[:, r, :], mT_low[:, r, c, :], high, start=False, stop=(c == C - 1))
                mm.then_inc(s_mup_ps, 1)

            def turn_mhid(t, r):
                pe.wait_ge(s_mhid, t + 1)
                if not isinstance(t, int) or t >= 2:
                    pe.wait_ge(s_mhT, t - 1)
                else:
                    pe.wait_ge(s_hid, G * UD)
                for c in range(C):
                    mm = pe.transpose(ps[:, 4 + r, P * c:P * c + P], mhid[:, r, P * c:P * c + P], ident[:])
                mm.then_inc(s_mhT_ps, 1)

            def mdown(t, r, e):
                pe.wait_ge(s_mhT, t + 1)
                if not isinstance(t, int) or t >= 2:
                    pe.wait_ge(s_z, t - 1)
                else:
                    pe.wait_ge(s_rt, PRIME + G * 2)
                    pe.wait_ge(s_wd, 16)
                for c in range(C):
                    mm = pe.matmul(ps[:, 6 + r, 0:D], mhidT[:, r, c, :], wd[:, bass.ds(e, 1), c, :].rearrange("p e i -> p (e i)"),
                                   start=(c == 0), stop=(c == C - 1))
                mm.then_inc(s_mdown, 1)

            def beat(b, four):
                r = four % 2
                if isinstance(b, int):
                    e_down = expert(b - 3) if real(b - 3) else None
                    e_up = expert(b) if real(b) else None
                else:
                    at = (four - (AHEAD - 1)) % 4
                    e_down, e_up = experts[at], experts[at + 3]
                if real(b - 3):
                    mdown(b - 3, 1 - r, e_down)
                if real(b - 2):
                    turn_mhid(b - 2, r)
                if real(b + 1):
                    turn_m(b + 1, 1 - r, (four + 1) % 4)
                if real(b):
                    mups(b, r, e_up)

            numbers = [pe.alloc_register(f"expert{i}") for i in range(7)]
            experts = []

            def read_experts(b):
                pe.load(numbers, tiles[0:1, 1, bass.ds(b - 3, len(numbers))])
                experts[:] = [pe.snap(e, min_val=0, max_val=E - 1) for e in numbers]

            tile_pipeline(pe, beat, read_experts)

        @block.vector
        def _(dve):
            dve.memset(chosen[:], 0.0).then_inc(s_setup, 1)
            dve.memset(v[0][0:SLOT], 0.0).then_inc(s_setup, 1)
            dve.memset(v[0][SLOT:P], 0.0).then_inc(s_setup, 1)
            dve.memset(v[1][0:SLOT], 0.0).then_inc(s_setup, 1)
            dve.memset(v[1][SLOT:P], 0.0).then_inc(s_setup, 1)
            dve.wait_ge(s_setup, 5)
            for a in range(2):
                for s in range(2):
                    ins = dve.memset(v[a][SLOT * s:SLOT * s + SLOT, :, :, s, HD:VW], 1.0)
            ins.then_inc(s_setup, 1)
            dve.wait_ge(s_w[0], 96)
            dve.tensor_scalar(qscale[:], colv[:, MEVEN:MEVEN + 2], QSCALE, None, ALU.mult).then_inc(s_const, 1)
            dve.tensor_copy(identr[:], ident[:]).then_inc(s_setup, 1)
            dve.tensor_copy(maskr[:], mask[:].unsqueeze(1).broadcast_to([P, C * R // 2, SLOT])).then_inc(s_setup, 1)
            dve.wait_ge(s_const, 3)
            for c in range(C):
                ins = dve.tensor_scalar(qbias[:, c, :], qscale[:], colv[:, BQ + c:BQ + c + 1], None, ALU.mult)
            ins.then_inc(s_setup, 1)
            dve.wait_ge(s_w[1], 16)
            for c in range(XC):
                at = P * (c % 2)
                fold = dve.scalar_tensor_tensor(out=convw[:, c, at:at + P], in0=ident[:], scalar=0.5,
                                                in1=convw[:, c, at:at + P], op0=ALU.mult, op1=ALU.add)
            fold.then_inc(s_fold, 1)
            dve.sem_inc(s_rt, PRIME)

            count = {"a": 0, "b": 0}

            def link(part, g, ins):
                count[part] += 1
                s, links = (s_order_a, LINKS_A) if part == "a" else (s_order_b, LINKS_B)
                ins.then_inc(s, 1)
                dve.wait_ge(s, g * links + count[part])

            def statistics(g, h):
                for j in range(T):
                    ins = dve.bn_stats(bst[:, j, :], h[:, j, :])
                link("a", g, ins)
                dve.memset(fence[:], 0.0)
                for j in range(T):
                    ins = dve.bn_aggr(mv[:, j, :], bst[:, j, :])
                ins.then_inc(s_var, 1)

            def normalise(g, k, h, dst):
                dve.wait_ge(s_rstd, g * 3 + k + 1)
                for j in range(T):
                    ins = dve.tensor_scalar(dst[:, j, :], h[:, j, :], mv[:, j, 0:1], rstd[:, j:j + 1],
                                            ALU.subtract, ALU.mult)
                    if k:
                        ins.then_inc(s_n, 1)
                return ins

            def before(a, g, j):
                k = 4 * a + j
                dve.wait_ge(s_s_ps, g * 8 + k + 1)
                both = ps[:, score_bank(a, g, j):score_bank(a, g, j) + 2, :]
                sp = both.rearrange("p s (r k) -> p s r k", k=SLOT)
                link("ab"[a], g, dve.tensor_reduce(mx[:, j % 2, :], both.rearrange("p s (r k) -> p (s r) k", k=SLOT), AX, ALU.max))
                past(dve, s_p, g * 8 + k)
                dve.tensor_tensor(scores[:, :, :, :].rearrange("p r s k -> p s r k"), sp,
                                  mx[:, j % 2, :].rearrange("p (s r) -> p s r", s=2).unsqueeze(3).broadcast_to([P, 2, C * R, SLOT]),
                                  ALU.subtract).then_inc(s_s_sub, 1)

            def after(a, g, j):
                k = 4 * a + j
                dve.wait_ge(s_pv, g * 16 + 2 * k + 2)
                ov = ps[:, 3, 0:H * VW].rearrange("p (h d) -> p h d", d=VW)
                link("ab"[a], g, dve.reciprocal(rinv[:], ov[:, :, HD]))
                ov = ov.rearrange("p (r s) d -> p r s d", s=2)
                dve.tensor_tensor(o[:, j, :, :].rearrange("p s (r d) -> p r s d", d=HD), ov[:, :, :, 0:HD],
                                  rinv[:].rearrange("p (r s) -> p r s", s=2).unsqueeze(3).broadcast_to([P, C * R, 2, HD]),
                                  ALU.mult).then_inc(s_o, 1)

            def evac_k(a, g):
                for c in range(C):
                    dve.wait_ge(s_k_ps, g * 4 + 2 * a + c + 1)
                    if a == 0:
                        dve.tensor_scalar(kT[a][:, :, c, :], ps[:, 4 + c, :].rearrange("p (j k) -> p j k", k=P),
                                          colv[:, BK + c:BK + c + 1], None, ALU.add)\
                           .then_inc(s_k, 1)
                    else:
                        dve.tensor_copy(kT[a][:, :, c, :], ps[:, 4 + c, :].rearrange("p (j k) -> p j k", k=P)).then_inc(s_k, 1)

            def hidden(g, i):
                dve.wait_ge(s_gate, g * UD + i + 1)
                link("b", g, dve.scalar_tensor_tensor(out=gate[:, i % 2, :], in0=gate[:, i % 2, :], scalar=1.0,
                                                      in1=ps[:, unit_bank(g, i), :], op0=ALU.add, op1=ALU.mult))
                if i >= 4:
                    dve.wait_ge(s_down, g * UD + i - 3)
                dve.scalar_tensor_tensor(out=hidT[:, i % 4, :], in0=gate[:, i % 2, :], scalar=0.5,
                                         in1=ps[:, unit_bank(g, i) + 1, :],
                                         op0=ALU.mult, op1=ALU.mult).then_inc(s_hid, 1)

            def scaled(g, k, bank, vec):
                dve.wait_ge(s_rms, g * 2 + k + 1)
                if k:
                    dve.wait_ge(s_y1, g + 1)
                elif isinstance(g, int):
                    dve.wait_ge(s_y, g)
                for j in range(T):
                    ins = dve.scalar_tensor_tensor(out=rt[:, j, :], in0=ps[:, bank + j // 2, D * (j % 2):D * (j % 2) + D],
                                                   scalar=rms[:, k, j:j + 1], in1=rowv[:, vec, :],
                                                   op0=ALU.mult, op1=ALU.mult)
                ins.then_inc(s_rt, 1)

            def conv_rows(g, tiles_of):
                for j in tiles_of:
                    dve.wait_ge(s_conv, g * T + j + 1)
                    ins = dve.tensor_tensor(h0[:, j, :], ps[:, 4 + j, 0:D], rowv[:, CONV_B, :], ALU.add)
                if j == T - 1:
                    link("a", g, ins)
                    statistics(g, h0)

            def scale(g):
                link("a", g, normalise(g, 0, h0, h0))
                link("a", g, dve.tensor_tensor(h0[:], h0[:], rowv[:, GAMMA:GAMMA + 1, :].broadcast_to([P, T, D]), ALU.mult))

            def shift(g):
                link("a", g, dve.tensor_tensor(h0[:], h0[:], rowv[:, BETA:BETA + 1, :].broadcast_to([P, T, D]), ALU.add))
                statistics(g, h0)

            def evac_v(g):
                for b in range(2):
                    dve.wait_ge(s_v_ps, g * 4 + b + 1)
                    for s in range(2):
                        rows = slice(SLOT * s, SLOT * s + SLOT)
                        bias = rowv[rows, BV, :].rearrange("p (h d) -> p h d", d=HD).unsqueeze(1)\
                            .broadcast_to([SLOT, 2, H, HD])
                        dve.tensor_tensor(v[0][rows, 2 * b:2 * b + 2, :, s, 0:HD],
                                          ps[rows, 6 + b, :].rearrange("p (j h d) -> p j h d", j=2, d=HD), bias,
                                          ALU.add).then_inc(s_v0, 1)

            def residual(g):
                dve.wait_ge(s_hbo, g + 1)
                past(dve, s_y0, g)
                for j in range(T):
                    dve.wait_ge(s_wo, g * 4 + j // 2 + 1)
                    ins = dve.tensor_tensor(h[:, j, :], ps[:, 2 + j // 2, D * (j % 2):D * (j % 2) + D], h0[:, j, :],
                                            ALU.add)
                link("a", g, ins)
                statistics(g, h)

            def route_max(g):
                dve.wait_ge(s_lg_ps, g + 1)
                lp = ps[:, 4, 0:T * E].rearrange("p (j e) -> p j e", e=E)
                link("a", g, dve.tensor_reduce(rs[:], lp, AX, ALU.max))
                dve.tensor_tensor(lg[:], lp, rs[:].unsqueeze(2).broadcast_to([P, T, E]), ALU.subtract)\
                   .then_inc(s_lgs, 1)

            def route_top(g):
                dve.wait_ge(s_lge, g + 1)
                link("b", g, dve.tensor_reduce(rs[:], lg[:], AX, ALU.add))
                link("b", g, dve.reciprocal(rs[:], rs[:]))
                link("b", g, dve.tensor_tensor(pr[:], lg[:], rs[:].unsqueeze(2).broadcast_to([P, T, E]), ALU.mult))
                other = pr[:].unsqueeze(2).broadcast_to([P, T, E, E])
                own = pr[:].unsqueeze(3).broadcast_to([P, T, E, E])
                dve.tensor_tensor(gt[:].rearrange("p (j e) f -> p j e f", e=E), other, own, ALU.is_gt)
                link("b", g, dve.tensor_tensor(eq[:].rearrange("p (j e) f -> p j e f", e=E), other, own, ALU.is_equal))
                ev = eq[:].rearrange("p (j e) f -> p j (e f)", e=E)
                link("b", g, dve.tensor_tensor(ev, ev, lower[:].unsqueeze(1).broadcast_to([P, T, E * E]), ALU.mult))
                link("b", g, dve.tensor_tensor(gt[:], gt[:], eq[:], ALU.add))
                link("b", g, dve.tensor_reduce(rank[:].rearrange("p j e -> p (j e)"), gt[:], AX, ALU.add))
                dve.tensor_scalar(chosen[:, 0:T, :], rank[:], 1.5, None, ALU.is_lt).then_inc(s_chosen, 1)
                dve.scalar_tensor_tensor(out=pick[:, 2, :, :], in0=rank[:], scalar=0.5,
                                         in1=marks[:, E:2 * E].unsqueeze(1).broadcast_to([P, T, E]),
                                         op0=ALU.is_lt, op1=ALU.mult)
                for k, op in ((0, ALU.is_lt), (1, ALU.is_equal)):
                    ins = dve.scalar_tensor_tensor(out=pick[:, 3 + k, :, :], in0=rank[:], scalar=(0.5, 1.0)[k], in1=pr[:],
                                                   op0=op, op1=ALU.mult)
                link("b", g, ins)
                dve.tensor_reduce(nx[:, :, FIRST:SENT].rearrange("p j k -> p k j"), pick[:, 2:5, :, :], AX, ALU.add)

            def take_places(g):
                dve.wait_ge(s_place, g + 1)
                counts = ps[:, 0, 0:(T + 1) * E].rearrange("p (j e) -> p j e", e=E)
                link("b", g, dve.tensor_tensor(place[:], counts[:, 0:T, :],
                                               filled[:].unsqueeze(1).broadcast_to([P, T, E]), ALU.add))
                dve.tensor_tensor(filled[:], filled[:], ps[:, 0, T * E:(T + 1) * E], ALU.add)\
                   .then_inc(s_placed, 1)
                for k, op in ((0, ALU.is_lt), (1, ALU.is_equal)):
                    ins = dve.scalar_tensor_tensor(out=pick[:, k, :, :], in0=rank[:], scalar=(0.5, 1.0)[k], in1=place[:],
                                                   op0=op, op1=ALU.mult)
                link("b", g, ins)
                link("b", g, dve.tensor_reduce(slotf[:], pick[:, 0:2, :, :], AX, ALU.add))
                dve.tensor_copy(slot_now[:], slotf[:]).then_inc(s_slot, 1)

            def list_tiles():
                steps = [0]

                def then(ins):
                    steps[0] += 1
                    ins.then_inc(s_order_t, 1)
                    dve.wait_ge(s_order_t, steps[0])

                dve.wait_ge(s_p, G * 8)
                dve.wait_ge(s_pT_ps, G * 16)
                t_own, t_val = (a[:].rearrange("p r s k -> p (r s k)")[:, 0:NT * E].rearrange("p (t e) -> p t e", e=E)
                                for a in (scores, probs))
                spare = scores[:].rearrange("p r s k -> p (r s k)")[:, NT * E:]
                many = spare[:, 0:E * 32].rearrange("p (e t) -> p e t", e=E)
                n_before = spare[:, E * 32:E * 32 + E * E].rearrange("p (e f) -> p e f", f=E)
                start, number = marks[:, 0:E], marks[:, E:2 * E]
                over, tile = marks[:, 2 * E:2 * E + 32], marks[:, 2 * E + 32:2 * E + 32 + NT]
                dve.wait_ge(s_placed, G)
                dve.tensor_copy(filledi[:], filled[:])
                then(dve.tensor_tensor(sent_n[:], filled[:], start, ALU.subtract))
                then(dve.tensor_tensor(many, sent_n[:].unsqueeze(2).broadcast_to([P, E, 32]),
                                       over.unsqueeze(1).broadcast_to([P, E, 32]), ALU.is_gt))
                then(dve.tensor_reduce(n_tiles[:], many, AX, ALU.add))
                then(dve.tensor_tensor(n_before, lower[:].rearrange("p (e f) -> p e f", f=E),
                                       n_tiles[:].unsqueeze(1).broadcast_to([P, E, E]), ALU.mult))
                then(dve.tensor_reduce(t_first[:], n_before, AX, ALU.add))
                dve.scalar_tensor_tensor(out=t_row[:], in0=t_first[:], scalar=float(-P), in1=start, op0=ALU.mult, op1=ALU.add)
                then(dve.tensor_tensor(t_end[:], t_first[:], n_tiles[:], ALU.add))

                def wide(a):
                    return a.unsqueeze(1).broadcast_to([P, NT, E])

                tile_w = tile.unsqueeze(2).broadcast_to([P, NT, E])
                dve.tensor_tensor(t_own, tile_w, wide(t_first[:]), ALU.is_ge)
                then(dve.tensor_tensor(t_val, tile_w, wide(t_end[:]), ALU.is_lt))
                then(dve.tensor_tensor(t_own, t_own, t_val, ALU.mult))
                then(dve.scalar_tensor_tensor(out=t_val, in0=tile_w, scalar=float(P), in1=wide(t_row[:]),
                                              op0=ALU.mult, op1=ALU.add))
                then(dve.tensor_tensor(t_val, t_val, t_own, ALU.mult))
                dve.tensor_reduce(tilesf[:, 0, :], t_val, AX, ALU.add)
                then(dve.tensor_tensor(t_own, t_own, wide(number), ALU.mult))
                then(dve.tensor_reduce(tilesf[:, 1, :], t_own, AX, ALU.add))
                dve.tensor_copy(tiles[:], tilesf[:]).then_inc(s_tiles, 1)
                dve.wait_ge(s_lg_ps, G)
                dve.wait_ge(s_lge, G)
                dve.wait_ge(s_rstd, G * 3)
                then(dve.memset(zero[:], 0.0))
                dve.tensor_copy(zero[:, ID:ID + 1], own[:, T:T + 1]).then_inc(s_zero, 1)

            def half(ga, gb):
                count["a"] = count["b"] = 0
                A, Bh = ga is not None, gb is not None
                if A:
                    for c in range(1, XC, 2):
                        dve.wait_ge(s_xt_ps, ga * XC + c + 1)
                        dve.tensor_copy(xT[:, c, :], ps[:, 4 + c, :]).then_inc(s_xt_v, 1)
                if Bh:
                    before(1, gb, 0)
                if A:
                    conv_rows(ga, (0,))
                for j in range(T):
                    if Bh and j + 1 < T:
                        before(1, gb, j + 1)
                    if A and j + 1 < T:
                        conv_rows(ga, (j + 1,))
                    if Bh:
                        after(1, gb, j)
                    if not A and j == 1:
                        route_top(gb)
                if A:
                    scale(ga)
                    shift(ga)
                    normalise(ga, 1, h0, n[0])
                if A and Bh:
                    route_top(gb)
                if not A:
                    take_places(gb)
                    list_tiles()
                if Bh:
                    scaled(gb, 0, 2, W_ATT)
                    dve.wait_ge(s_rt, PRIME + gb * 2 + 1)
                    dve.tensor_tensor(hd[:], rt[:], n[1][:], ALU.add).then_inc(s_hd, 1)
                if A and Bh:
                    take_places(gb)
                if A:
                    evac_k(0, ga)
                if A:
                    evac_v(ga)
                if Bh:
                    for c in range(C):
                        dve.wait_ge(s_hdT_a, gb * 2 + c + 1)
                        dve.tensor_tensor(hdT_low[:, c, :], ps[:, 4 + c, :], hdT[:, c, :].bitcast(F32), ALU.subtract)\
                           .then_inc(s_hdT_low, 1)
                if A:
                    before(0, ga, 0)
                if A and not Bh:
                    dve.wait_ge(s_w[3], 80)
                    dve.tensor_copy(filled[:], marks[:, 0:E])
                if Bh:
                    hidden(gb, 0)
                for j in range(T):
                    if A and j + 1 < T:
                        before(0, ga, j + 1)
                    if Bh:
                        hidden(gb, j + 1)
                    if A:
                        after(0, ga, j)
                if Bh:
                    hidden(gb, 5)
                if A:
                    residual(ga)
                if Bh:
                    hidden(gb, 6)
                if A:
                    past(dve, s_sent, ga * (2 * T * 16))
                    if Bh:
                        dve.tensor_scalar(nx[:, :, ID], nx[:, :, ID], float(2 * GT), None, ALU.add)
                    else:
                        dve.tensor_copy(nx[:, :, ID], own[:, 0:T])
                    normalise(ga, 2, h, n[1])
                if Bh:
                    hidden(gb, 7)
                    scaled(gb, 1, 6, W_FF)
                if A:
                    evac_k(1, ga)
                    route_max(ga)
                assert not A or count["a"] == LINKS_A, count
                assert not Bh or count["b"] == LINKS_B, count

            pipeline(dve, half)

            attention_ended(dve)

            def at(t):
                return slice(t, t + 1) if isinstance(t, int) else bass.ds(t, 1)

            def number(t):
                return tilesf[:, 1, at(t)]

            def half_of(t, r):
                return (t - r) // 2

            def beat(b, four):
                r = four % 2
                if real(b + 1):
                    q, k = 1 - r, (four + 1) % 4
                    dve.wait_ge(s_m[k], quarter(b + 1, k))
                    dve.tensor_copy(meta[:, at(b + 1), :], m[:, k, ID:SENT]).then_inc(s_meta, 1)
                if real(b + 1):
                    dve.wait_ge(s_mT, b + 2)
                    if not isinstance(b, int) or b >= 1:
                        dve.wait_ge(s_mup_ps, b)
                    dve.tensor_tensor(mT_low[:, q, :, :].rearrange("p c k -> p (c k)"), ps[:, 2 + q, 0:D],
                                      mT[:, q, :, :].rearrange("p c k -> p (c k)").bitcast(F32), ALU.subtract)\
                       .then_inc(s_mT_low, 1)
                if real(b):
                    dve.wait_ge(s_mgate, b + 1)
                    dve.scalar_tensor_tensor(out=mup[:, r, :], in0=mgate[:, r, :], scalar=1.0, in1=ps[:, r, 0:D],
                                             op0=ALU.add, op1=ALU.mult).then_inc(s_mu, 1)
                    dve.wait_ge(s_mu, b + 1)
                    if not isinstance(b, int) or b >= 2:
                        dve.wait_ge(s_mhT_ps, b - 1)
                    dve.scalar_tensor_tensor(out=mhid[:, r, :], in0=mup[:, r, :], scalar=0.5, in1=ps[:, r, D:2 * D],
                                             op0=ALU.mult, op1=ALU.mult).then_inc(s_mhid, 1)

                if real(b - 2):
                    t = b - 2
                    if not isinstance(b, int) or b >= 4:
                        dve.wait_ge(s_z, b - 3)
                    for k, op in ((0, ALU.is_equal), (1, ALU.not_equal)):
                        ins = dve.scalar_tensor_tensor(out=parts[:, r, k:k + 1], in0=meta[:, at(t), 1:2],
                                                       scalar=number(t), in1=meta[:, at(t), 2 + k:3 + k],
                                                       op0=op, op1=ALU.mult)
                    ins.then_inc(s_parts, 1)
                    dve.wait_ge(s_parts, b - 1)
                    dve.tensor_tensor(portion[:, r:r + 1], parts[:, r, 0:1], parts[:, r, 1:2], ALU.add)\
                       .then_inc(s_portion, 1)
                if real(b - 3):
                    k, t = (four - 3) % 4, b - 3
                    if not isinstance(b, int) or b >= 7:
                        dve.wait_ge(s_back[k], quarter(t - 4, k))
                    dve.scalar_tensor_tensor(out=target[:, k:k + 1], in0=meta[:, at(t), 1:2], scalar=number(t),
                                             in1=meta[:, at(t), 0:1], op0=ALU.not_equal, op1=ALU.add).then_inc(s_target, 1)

            tile_pipeline(dve, beat)

            first_phase_ended(dve)
            dve.wait_ge(s_yin, G * T * 16)

            def join(g, r, first):
                dve.wait_ge(s_got[r], half_of(g, r) * 16 + 16)
                if not first:
                    dve.wait_ge(s_my, g - 1)
                dve.tensor_tensor(moe[:, r, :, :], zg[:, r, :, 0, :], zg[:, r, :, 1, :], ALU.add).then_inc(s_moe, 1)

            def finish(g, r):
                dve.wait_ge(s_mrms, g + 1)
                for j in range(T):
                    ins = dve.scalar_tensor_tensor(out=moe2[:, r, j, :], in0=moe[:, r, j, :], scalar=mrms[:, r, j:j + 1],
                                                   in1=rowv[:, W_MOE, :], op0=ALU.mult, op1=ALU.mult)
                ins.then_inc(s_mt, 1)
                dve.wait_ge(s_mt, g + 1)
                to = my[:, bass.ds(g * T, T), :]
                dve.tensor_tensor(to, to, moe2[:, r, :, :], ALU.add).then_inc(s_my, 1)

            for r in range(2):
                join(r, r, True)
            with dve.Fori(0, G // 2 - 1) as i:
                for r in range(2):
                    finish(2 * i + r, r)
                    join(2 * i + r + 2, r, False)
            for r in range(2):
                finish(G - 2 + r, r)


def kernel(x, L0_tok_conv_w, L0_tok_conv_b, L0_tok_ln_gamma, L0_tok_ln_beta, L0_attn_Wq, L0_attn_bq, L0_attn_Wk,
           L0_attn_bk, L0_attn_Wv, L0_attn_bv, L0_attn_Wo, L0_attn_bo, L0_ffn_wq, L0_ffn_wk, L0_ffn_wv, L0_ffn_wo,
           L0_ffn_w1, L0_ffn_w2, L0_ffn_w3, L0_ffn_attn_norm_w, L0_ffn_ff_norm_w, L0_ffn_moe_norm_w, L0_ffn_router_w,
           L0_ffn_ew1, L0_ffn_ew2, L0_ffn_ew3):
    import numpy as np
    import concourse.bacc as bacc
    from concourse.bass_utils import run_bass_kernel_spmd

    def contraction_first(w):
        w = np.asarray(w)
        w = w.reshape(w.shape[:-2] + (w.shape[-2] // P, P, w.shape[-1]))
        return np.ascontiguousarray(np.moveaxis(w, -2, 0))

    def by_parity(w):
        return np.asarray(w).reshape(C * R, 2, HD, D).transpose(1, 0, 2, 3).reshape(D, D)

    def per_feature(b):
        return np.asarray(b).reshape(C, P).T

    rows = np.stack([np.asarray(b) for b in (L0_tok_conv_b, L0_tok_ln_gamma, L0_tok_ln_beta, L0_attn_bv, L0_attn_bo,
                                             L0_ffn_attn_norm_w, L0_ffn_ff_norm_w, L0_ffn_moe_norm_w)])
    even = (np.arange(P) % 32 < HD).astype(np.float32)[:, None]
    row = np.arange(P)[:, None] % SLOT
    pair = (np.arange(P)[:, None] // 32 == np.arange(R)[None, :]).astype(np.float32)
    start = P + np.arange(E) * CAP
    marks = np.concatenate([start, np.arange(E), P * np.arange(32), np.arange(NT)]).astype(np.float32)
    own = 2 * np.concatenate([np.arange(P)[:, None] * T + np.arange(T), B * SLOT + np.arange(P)[:, None]], axis=1)
    before = np.stack([np.triu(np.ones((P, P), np.float32), 1), np.ones((P, P), np.float32)], axis=1)
    arrays = {
        "x": np.asarray(x).reshape(G, T, 2, L, D),
        "rows": np.ascontiguousarray(np.broadcast_to(rows, (P,) + rows.shape)),
        "cols": np.concatenate([per_feature(L0_attn_bq), per_feature(L0_attn_bk), even, 1 - even, pair], axis=1),
        "ident": np.eye(P, dtype=np.float32),
        "mask": np.where(np.arange(SLOT)[None, :] <= row, 0.0, NEG).astype(np.float32),
        "lower": np.ascontiguousarray(np.broadcast_to(np.tril(np.ones((E, E), np.float32), -1).reshape(1, -1), (P, E * E))),
        "before": before,
        "marks": np.ascontiguousarray(np.broadcast_to(marks, (P, marks.size))),
        "own": own.astype(np.float32),
        "conv_w": contraction_first(np.asarray(L0_tok_conv_w).transpose(2, 1, 0).reshape(2 * D, D)),
        "attn_w": contraction_first(np.stack([np.asarray(w).T for w in (L0_attn_Wq, L0_attn_Wk, L0_attn_Wv)]
                                             + [by_parity(np.asarray(L0_attn_Wo).T)]
                                             + [np.asarray(w) for w in (L0_ffn_wq, L0_ffn_wk, L0_ffn_wv)]
                                             + [by_parity(L0_ffn_wo)])),
        "w1": contraction_first(L0_ffn_w1),
        "w3": contraction_first(L0_ffn_w3),
        "w2": contraction_first(L0_ffn_w2),
        "router": contraction_first(L0_ffn_router_w),
        "ew13": contraction_first(np.concatenate([np.asarray(L0_ffn_ew1), np.asarray(L0_ffn_ew3)], axis=-1)),
        "ew2": contraction_first(L0_ffn_ew2),
    }
    nc = bacc.Bacc("TRN2", target_bir_lowering=False, num_devices=1)
    arrays = {f"in_{k}": np.ascontiguousarray(a) for k, a in arrays.items()}
    aps = [nc.dram_tensor(k, a.shape, F32, kind="ExternalInput").ap() for k, a in arrays.items()]
    out = nc.dram_tensor("out", (G, T, 2, TOK, D), F32, kind="ExternalOutput").ap()
    program(nc, *aps, out)
    r = run_bass_kernel_spmd(nc, [arrays], core_ids=[0])
    return r.results[0]["out"].reshape(B, TOK, D)
```
